# Optimizing a Trainium2 kernel written in Bass

```python
import numpy as np
import jax
import jax.numpy as jnp

def _softmax(x, axis=-1):
    return jax.nn.softmax(x, axis=axis)

def _gelu(x):
    return jax.nn.gelu(x, approximate=True)

def _silu(x):
    return jax.nn.silu(x)

def _sigmoid(x):
    return jax.nn.sigmoid(x)

def _layernorm(x, axis=-1, eps=1e-05):
    m = jnp.mean(x, axis=axis, keepdims=True)
    v = jnp.var(x, axis=axis, keepdims=True)
    return (x - m) / jnp.sqrt(v + eps)

def _scatter_add(tgt, idx, src, axis=0):
    return tgt.at[idx].add(src)

def _segment_sum(src, seg, n):
    return jax.ops.segment_sum(src, seg, n)
kernel_name = 'mk_seq_preln_d1_jaxref_r8_d6c5cf'

def setup_inputs(seed: int=0):
    np.random.seed(seed)
    _w = jnp.asarray

    def _L0_attn_setup():
        import jax, jax.numpy as jnp
        import numpy as np
        DIM = 128
        NUM_HEADS = 16
        HEAD_DIM = DIM // NUM_HEADS
        SCALE = HEAD_DIM ** (-0.5)
        WINDOW = 32
        EXT = WINDOW // 2
        B, N = (4, 512)

        def _local_attention(x, w_qkv, b_qkv, w_proj, b_proj):
            b, n, c = x.shape
            h, hd, w, e = (NUM_HEADS, HEAD_DIM, WINDOW, EXT)
            g = n // w
            kw_len = w + 2 * e
            qkv = (x @ w_qkv.T + b_qkv).reshape(b, n, 3, h, hd).transpose(2, 0, 3, 1, 4)
            q, k, v = (qkv[0], qkv[1], qkv[2])
            qw = q.reshape(b, h, g, w, hd)
            kp = jnp.pad(k, ((0, 0), (0, 0), (e, e), (0, 0)))
            vp = jnp.pad(v, ((0, 0), (0, 0), (e, e), (0, 0)))
            idx = jnp.arange(g)[:, None] * w + jnp.arange(kw_len)[None, :]
            kw = kp[:, :, idx]
            vw = vp[:, :, idx]
            dots = jnp.einsum('bhgqd,bhgkd->bhgqk', qw, kw) * SCALE
            pos = idx - e
            valid = (pos >= 0) & (pos < n)
            dots = jnp.where(valid[None, None, :, None, :], dots, -jnp.inf)
            attn = jax.nn.softmax(dots, axis=-1)
            out = jnp.einsum('bhgqk,bhgkd->bhgqd', attn, vw)
            out = out.reshape(b, h, n, hd).transpose(0, 2, 1, 3).reshape(b, n, c)
            return out @ w_proj.T + b_proj
        key = jax.random.key(seed)
        ks = jax.random.split(key, 5)
        x = jax.random.normal(ks[0], (B, N, DIM), dtype=jnp.float32)
        w_qkv = jax.random.normal(ks[1], (3 * DIM, DIM), dtype=jnp.float32) * 0.02
        b_qkv = jnp.zeros((3 * DIM,), dtype=jnp.float32)
        w_proj = jax.random.normal(ks[2], (DIM, DIM), dtype=jnp.float32) * 0.02
        b_proj = jnp.zeros((DIM,), dtype=jnp.float32)
        return {'x': x, 'w_qkv': w_qkv, 'b_qkv': b_qkv, 'w_proj': w_proj, 'b_proj': b_proj}
    _L0_attn_in = _L0_attn_setup()

    def _L0_ffn_setup():
        import jax, jax.numpy as jnp
        import numpy as np
        DIM = 128
        DEPTH = 6
        HEADS = 16
        DIM_HEAD = 64
        WINDOW = 32
        INNER = HEADS * DIM_HEAD
        DIM_INNER = int(DIM * 4 * 2 / 3)
        QK_SCALE = 8.0

        def shift_tokens(t):
            a, s = jnp.split(t, 2, -1)
            s = jnp.pad(s, ((0, 0), (1, 0), (0, 0)))[:, :-1]
            return jnp.concatenate([a, s], -1)

        def l2norm(t):
            return t / jnp.maximum(jnp.linalg.norm(t, axis=-1, keepdims=True), 1e-12)

        def rotate_half(x):
            x1, x2 = jnp.split(x, 2, -1)
            return jnp.concatenate([-x2, x1], -1)

        def rotary_tables(n):
            half = jnp.arange(0, DIM_HEAD, 2, dtype=jnp.float32)
            inv_freq = 1.0 / 10000.0 ** (half / DIM_HEAD)
            t = jnp.arange(n, dtype=jnp.float32)
            freqs = t[:, None] * inv_freq[None, :]
            freqs = jnp.concatenate([freqs, freqs], -1)
            base_scale = (half + 0.4 * DIM_HEAD) / (1.4 * DIM_HEAD)
            power = (t - n // 2) / (WINDOW // 2)
            scale = base_scale[None, :] ** power[:, None]
            scale = jnp.concatenate([scale, scale], -1)
            return (freqs, scale)

        def local_attention(q, k, v):
            b, h, n, d = q.shape
            w = WINDOW
            nw = n // w
            bq = q.reshape(b, h, nw, w, d)
            bk = k.reshape(b, h, nw, w, d)
            bv = v.reshape(b, h, nw, w, d)

            def look(t):
                p = jnp.pad(t, ((0, 0), (0, 0), (1, 0), (0, 0), (0, 0)))
                return jnp.concatenate([p[:, :, :nw], p[:, :, 1:]], axis=3)
            bk2, bv2 = (look(bk), look(bv))
            seq = jnp.arange(n).reshape(nw, w)
            seq_p = jnp.pad(seq, ((1, 0), (0, 0)), constant_values=-1)
            jt = jnp.concatenate([seq_p[:nw], seq_p[1:]], axis=1)
            it = seq[:, :, None]
            jb = jt[:, None, :]
            mask = (it < jb) | (it > jb + w) | (jb == -1)
            sim = jnp.einsum('bhwie,bhwje->bhwij', bq, bk2) * QK_SCALE
            sim = jnp.where(mask, -jnp.finfo(sim.dtype).max, sim)
            attn = jax.nn.softmax(sim, -1)
            out = jnp.einsum('bhwij,bhwje->bhwie', attn, bv2)
            return out.reshape(b, h, n, d)

        def attn_layer(x, Wqkv, qs, ksc, Wo):
            b, n, _ = x.shape
            qkv = x @ Wqkv
            q, k, v = jnp.split(qkv, 3, -1)
            sh = lambda t: t.reshape(b, n, HEADS, DIM_HEAD).transpose(0, 2, 1, 3)
            q, k, v = (sh(q), sh(k), sh(v))
            q = l2norm(q) * qs
            k = l2norm(k) * ksc
            freqs, scale = rotary_tables(n)
            cos, sin = (jnp.cos(freqs), jnp.sin(freqs))
            q = q * cos * scale + rotate_half(q) * sin * scale
            inv = 1.0 / scale
            k = k * cos * inv + rotate_half(k) * sin * inv
            out = local_attention(q, k, v)
            out = out.transpose(0, 2, 1, 3).reshape(b, n, INNER)
            return out @ Wo

        def ffn_layer(x, g, bln, W1, b1, W2, b2):
            mu = x.mean(-1, keepdims=True)
            var = ((x - mu) ** 2).mean(-1, keepdims=True)
            xn = (x - mu) / jnp.sqrt(var + 1e-05) * g + bln
            hg = xn @ W1 + b1
            a, gate = jnp.split(hg, 2, -1)
            return a * jax.nn.gelu(gate, approximate=False) @ W2 + b2
        key = jax.random.key(seed)
        ks = jax.random.split(key, 8)
        B, N = (2, 256)
        init = lambda k, shape: jax.random.normal(k, shape, jnp.float32) * 0.02
        return {'x': jax.random.normal(ks[0], (B, N, DIM), jnp.float32), 'Wqkv': init(ks[1], (DEPTH, DIM, 3 * INNER)), 'q_scale': jnp.ones((DEPTH, DIM_HEAD), jnp.float32), 'k_scale': jnp.ones((DEPTH, DIM_HEAD), jnp.float32), 'Wo': init(ks[2], (DEPTH, INNER, DIM)), 'ln_g': jnp.ones((DEPTH, DIM), jnp.float32), 'ln_b': jnp.zeros((DEPTH, DIM), jnp.float32), 'W1': init(ks[3], (DEPTH, DIM, 2 * DIM_INNER)), 'b1': jnp.zeros((DEPTH, 2 * DIM_INNER), jnp.float32), 'W2': init(ks[4], (DEPTH, DIM_INNER, DIM)), 'b2': jnp.zeros((DEPTH, DIM), jnp.float32)}
    _L0_ffn_in = _L0_ffn_setup()
    _d = {'L0_attn_x': _L0_attn_in['x'], 'L0_attn_w_qkv': _L0_attn_in['w_qkv'], 'L0_attn_b_qkv': _L0_attn_in['b_qkv'], 'L0_attn_w_proj': _L0_attn_in['w_proj'], 'L0_attn_b_proj': _L0_attn_in['b_proj'], 'L0_ffn_Wqkv': _L0_ffn_in['Wqkv'], 'L0_ffn_q_scale': _L0_ffn_in['q_scale'], 'L0_ffn_k_scale': _L0_ffn_in['k_scale'], 'L0_ffn_Wo': _L0_ffn_in['Wo'], 'L0_ffn_ln_g': _L0_ffn_in['ln_g'], 'L0_ffn_ln_b': _L0_ffn_in['ln_b'], 'L0_ffn_W1': _L0_ffn_in['W1'], 'L0_ffn_b1': _L0_ffn_in['b1'], 'L0_ffn_W2': _L0_ffn_in['W2'], 'L0_ffn_b2': _L0_ffn_in['b2']}
    _x0 = _d['L0_attn_x']
    _d['L0_attn_x'] = jax.random.normal(jax.random.fold_in(jax.random.key(seed), 1), (16, 256, 128), dtype=_x0.dtype)
    del _x0
    return _d

def reference(L0_attn_x, L0_attn_w_qkv, L0_attn_b_qkv, L0_attn_w_proj, L0_attn_b_proj, L0_ffn_Wqkv, L0_ffn_q_scale, L0_ffn_k_scale, L0_ffn_Wo, L0_ffn_ln_g, L0_ffn_ln_b, L0_ffn_W1, L0_ffn_b1, L0_ffn_W2, L0_ffn_b2):

    def _L0_attn_ref(x, w_qkv, b_qkv, w_proj, b_proj):
        import jax, jax.numpy as jnp
        import numpy as np
        DIM = 128
        NUM_HEADS = 16
        HEAD_DIM = DIM // NUM_HEADS
        SCALE = HEAD_DIM ** (-0.5)
        WINDOW = 32
        EXT = WINDOW // 2
        B, N = (4, 512)

        def _local_attention(x, w_qkv, b_qkv, w_proj, b_proj):
            b, n, c = x.shape
            h, hd, w, e = (NUM_HEADS, HEAD_DIM, WINDOW, EXT)
            g = n // w
            kw_len = w + 2 * e
            qkv = (x @ w_qkv.T + b_qkv).reshape(b, n, 3, h, hd).transpose(2, 0, 3, 1, 4)
            q, k, v = (qkv[0], qkv[1], qkv[2])
            qw = q.reshape(b, h, g, w, hd)
            kp = jnp.pad(k, ((0, 0), (0, 0), (e, e), (0, 0)))
            vp = jnp.pad(v, ((0, 0), (0, 0), (e, e), (0, 0)))
            idx = jnp.arange(g)[:, None] * w + jnp.arange(kw_len)[None, :]
            kw = kp[:, :, idx]
            vw = vp[:, :, idx]
            dots = jnp.einsum('bhgqd,bhgkd->bhgqk', qw, kw) * SCALE
            pos = idx - e
            valid = (pos >= 0) & (pos < n)
            dots = jnp.where(valid[None, None, :, None, :], dots, -jnp.inf)
            attn = jax.nn.softmax(dots, axis=-1)
            out = jnp.einsum('bhgqk,bhgkd->bhgqd', attn, vw)
            out = out.reshape(b, h, n, hd).transpose(0, 2, 1, 3).reshape(b, n, c)
            return out @ w_proj.T + b_proj
        return _local_attention(x, w_qkv, b_qkv, w_proj, b_proj)

    def _L0_ffn_ref(x, Wqkv, q_scale, k_scale, Wo, ln_g, ln_b, W1, b1, W2, b2):
        import jax, jax.numpy as jnp
        import numpy as np
        DIM = 128
        DEPTH = 6
        HEADS = 16
        DIM_HEAD = 64
        WINDOW = 32
        INNER = HEADS * DIM_HEAD
        DIM_INNER = int(DIM * 4 * 2 / 3)
        QK_SCALE = 8.0

        def shift_tokens(t):
            a, s = jnp.split(t, 2, -1)
            s = jnp.pad(s, ((0, 0), (1, 0), (0, 0)))[:, :-1]
            return jnp.concatenate([a, s], -1)

        def l2norm(t):
            return t / jnp.maximum(jnp.linalg.norm(t, axis=-1, keepdims=True), 1e-12)

        def rotate_half(x):
            x1, x2 = jnp.split(x, 2, -1)
            return jnp.concatenate([-x2, x1], -1)

        def rotary_tables(n):
            half = jnp.arange(0, DIM_HEAD, 2, dtype=jnp.float32)
            inv_freq = 1.0 / 10000.0 ** (half / DIM_HEAD)
            t = jnp.arange(n, dtype=jnp.float32)
            freqs = t[:, None] * inv_freq[None, :]
            freqs = jnp.concatenate([freqs, freqs], -1)
            base_scale = (half + 0.4 * DIM_HEAD) / (1.4 * DIM_HEAD)
            power = (t - n // 2) / (WINDOW // 2)
            scale = base_scale[None, :] ** power[:, None]
            scale = jnp.concatenate([scale, scale], -1)
            return (freqs, scale)

        def local_attention(q, k, v):
            b, h, n, d = q.shape
            w = WINDOW
            nw = n // w
            bq = q.reshape(b, h, nw, w, d)
            bk = k.reshape(b, h, nw, w, d)
            bv = v.reshape(b, h, nw, w, d)

            def look(t):
                p = jnp.pad(t, ((0, 0), (0, 0), (1, 0), (0, 0), (0, 0)))
                return jnp.concatenate([p[:, :, :nw], p[:, :, 1:]], axis=3)
            bk2, bv2 = (look(bk), look(bv))
            seq = jnp.arange(n).reshape(nw, w)
            seq_p = jnp.pad(seq, ((1, 0), (0, 0)), constant_values=-1)
            jt = jnp.concatenate([seq_p[:nw], seq_p[1:]], axis=1)
            it = seq[:, :, None]
            jb = jt[:, None, :]
            mask = (it < jb) | (it > jb + w) | (jb == -1)
            sim = jnp.einsum('bhwie,bhwje->bhwij', bq, bk2) * QK_SCALE
            sim = jnp.where(mask, -jnp.finfo(sim.dtype).max, sim)
            attn = jax.nn.softmax(sim, -1)
            out = jnp.einsum('bhwij,bhwje->bhwie', attn, bv2)
            return out.reshape(b, h, n, d)

        def attn_layer(x, Wqkv, qs, ksc, Wo):
            b, n, _ = x.shape
            qkv = x @ Wqkv
            q, k, v = jnp.split(qkv, 3, -1)
            sh = lambda t: t.reshape(b, n, HEADS, DIM_HEAD).transpose(0, 2, 1, 3)
            q, k, v = (sh(q), sh(k), sh(v))
            q = l2norm(q) * qs
            k = l2norm(k) * ksc
            freqs, scale = rotary_tables(n)
            cos, sin = (jnp.cos(freqs), jnp.sin(freqs))
            q = q * cos * scale + rotate_half(q) * sin * scale
            inv = 1.0 / scale
            k = k * cos * inv + rotate_half(k) * sin * inv
            out = local_attention(q, k, v)
            out = out.transpose(0, 2, 1, 3).reshape(b, n, INNER)
            return out @ Wo

        def ffn_layer(x, g, bln, W1, b1, W2, b2):
            mu = x.mean(-1, keepdims=True)
            var = ((x - mu) ** 2).mean(-1, keepdims=True)
            xn = (x - mu) / jnp.sqrt(var + 1e-05) * g + bln
            hg = xn @ W1 + b1
            a, gate = jnp.split(hg, 2, -1)
            return a * jax.nn.gelu(gate, approximate=False) @ W2 + b2
        for i in range(DEPTH):
            x = attn_layer(shift_tokens(x), Wqkv[i], q_scale[i], k_scale[i], Wo[i]) + x
            x = ffn_layer(shift_tokens(x), ln_g[i], ln_b[i], W1[i], b1[i], W2[i], b2[i]) + x
        return x
    x = L0_attn_x
    x = x + _L0_attn_ref(_layernorm(x, axis=-1), L0_attn_w_qkv, L0_attn_b_qkv, L0_attn_w_proj, L0_attn_b_proj)
    x = x + _L0_ffn_ref(_layernorm(x, axis=-1), L0_ffn_Wqkv, L0_ffn_q_scale, L0_ffn_k_scale, L0_ffn_Wo, L0_ffn_ln_g, L0_ffn_ln_b, L0_ffn_W1, L0_ffn_b1, L0_ffn_W2, L0_ffn_b2)
    return x

_drawn_inputs = setup_inputs


def setup_inputs(seed=0):
    import zlib

    import numpy as np

    out = dict(_drawn_inputs(seed))
    spreads = {'L0_attn_b_qkv': (0.0, 0.312),
     'L0_attn_b_proj': (0.0, 0.1),
     'L0_ffn_q_scale': (1.0, 0.6),
     'L0_ffn_k_scale': (1.0, 0.6),
     'L0_ffn_ln_g': (1.0, 0.6),
     'L0_ffn_ln_b': (0.0, 0.8),
     'L0_ffn_b1': (0.0, 0.8),
     'L0_ffn_b2': (0.0, 0.1)}
    factors = {'L0_attn_w_qkv': 8.0, 'L0_ffn_W1': 3.643, 'L0_ffn_W2': 3.567}
    for name, (base, spread) in spreads.items():
        noise = np.random.default_rng([zlib.crc32(name.encode()), seed]).standard_normal(out[name].shape)
        drawn = base * np.exp(spread * noise) if base else spread * noise
        out[name] = jnp.asarray(drawn.astype(out[name].dtype))
    for name, factor in factors.items():
        out[name] = (out[name] * factor).astype(out[name].dtype)
    return out
```

```python
from contextlib import ExitStack

import numpy as np

import concourse.bass as bass
from concourse import mybir

ALU = mybir.AluOpType
ACT = mybir.ActivationFunctionType
F32 = mybir.dt.float32
BF16 = mybir.dt.bfloat16
I32 = mybir.dt.int32
AX_X = mybir.AxisListType.X

P = 128
SEQS, N_TOK, DIM = 16, 256, 128
TOKENS = SEQS * N_TOK
DEPTH = 6
HEADS, DIM_HEAD = 16, 64
INNER = HEADS * DIM_HEAD
DIM_INNER = int(DIM * 4 * 2 / 3)
HEAD_DIM0 = DIM // HEADS
SCALE0 = HEAD_DIM0 ** -0.5
QK_SCALE = 8.0
WINDOW = 32
BLOCK_Q = 64
BLOCK_K = BLOCK_Q + WINDOW
BLOCKS = N_TOK // BLOCK_Q
PADDED = N_TOK + WINDOW
QUADS = 8
UNIT = 512
UNITS = TOKENS // UNIT
LN_EPS = 1e-5
RSQRT_MAGIC = 1597463007.0
NEWTON_OPS = 11
FIRST_N = 2
F_CHUNKS = [(c * P, min(P, DIM_INNER - c * P)) for c in range(-(-DIM_INNER // P))]
NF = len(F_CHUNKS)

DEEP_STEPS = [
    [("PJ", 0), ("PJ", 1)],
    [("PJ", 2), ("PJ", 3), ("V", 0)],
    [("PJ", 4), ("V", 1)],
    [("PJ", 5), ("TQ", 0), ("V", 2)],
    [("PJ", 6), ("TQ", 1)],
    [("PJ", 7), ("TQ", 2), ("V", 3)],
    [("TK", 0), ("TQ", 3), ("V", 4)],
    [("TK", 1), ("V", 5)],
    [("TK", 2), ("TK", 3), ("V", 6)],
    [("V", 7)],
]
FIRST_STEPS = [[("Q", 0)], [("K", 0)], [("V0", 0)], [("V0", 1)], [("V0", 2)], [("V0", 3)], [], [], [], []]
STEPS = QUADS + 2


class Geometry:

    def __init__(self, first):
        self.first = first
        self.steps = FIRST_STEPS if first else DEEP_STEPS
        order = [item for step in self.steps for item in step]
        assert len(order) % 3 == 0
        self.index = {item: j for j, item in enumerate(order)}
        self.items = len(order)
        self.quads_per_out = 4 if first else 2
        self.outs = QUADS // self.quads_per_out
        self.chunks = 1 if first else INNER // P
        self.lead = WINDOW // 2 if first else WINDOW


class Buffers:
    pass


def counts(e, n, pers):
    if isinstance(n, int):
        return {per: n * per for per in pers}
    return {per: (e.snap(n * per) if per > 1 else n) for per in pers}


def bf16_parts_matmul(e, out, stat, moving, start, stop, skip=False):
    (sh, sl), (mh, ml) = stat, moving
    e.matmul(out, sh, mh, start=start, stop=False, skip_group_check=skip)
    e.matmul(out, sh, ml, start=False, stop=False, skip_group_check=skip)
    return e.matmul(out, sl, mh, start=False, stop=stop, skip_group_check=skip)


def rsqrt_op(e, i, x, y, a, src, floor, scale):
    if i == 0:
        return e.tensor_scalar(x, src, floor, scale, ALU.max, ALU.mult)
    if i == 1:
        return e.tensor_scalar(y.bitcast(I32), x.bitcast(I32), -0.5, RSQRT_MAGIC, ALU.mult, ALU.add)
    if i % 3 == 2:
        return e.tensor_tensor(a, y, y, ALU.mult)
    if i % 3 == 0:
        return e.scalar_tensor_tensor(a, a, -0.5, x, ALU.mult, ALU.mult)
    return e.scalar_tensor_tensor(y, a, 1.5, y, ALU.add, ALU.mult)


def quad_heads(g, m):
    t, quad = divmod(m, 4)
    if g.first:
        return t, 32 * quad, 32, [(r, 4 * quad + r) for r in range(4)]
    half, odd = divmod(quad, 2)
    return t, 64 * odd, 64, [(4 * half + j, 8 * half + 2 * j + odd) for j in range(4)]



class AttentionSems:

    def __init__(self, ctx, nc, tag):
        def sem(name):
            return ctx.enter_context(nc.semaphore(f"{tag}_{name}"))

        self.x_hi = sem("x_hi")
        self.x_lo = sem("x_lo")
        self.work_full = sem("work_full")
        self.work_read = sem("work_read")
        self.work_free = sem("work_free")
        self.rotated = sem("rotated")
        self.newton = sem("newton")
        self.k_scaled = sem("k_scaled")
        self.scores = sem("scores")
        self.row_max = sem("row_max")
        self.neg_max = sem("neg_max")
        self.exps = sem("exps")
        self.recip = sem("recip")
        self.probs = sem("probs")
        self.pt_full = sem("pt_full")
        self.pt_hi = sem("pt_hi")
        self.pt_lo = sem("pt_lo")
        self.pv_full = sem("pv_full")
        self.out_hi = sem("out_hi")
        self.out_lo = sem("out_lo")
        self.proj_full = sem("proj_full")
        self.residual = sem("residual")
        self.v_sum = sem("v_sum")
        self.q_sum = sem("q_sum")


def pe_credit(e, g, s):
    e.sem_inc(s.work_full, FIRST_N * g.items)
    e.sem_inc(s.scores, FIRST_N * 8)
    e.sem_inc(s.pt_full, FIRST_N * 8)
    e.sem_inc(s.pv_full, FIRST_N * 8)
    e.sem_inc(s.proj_full, FIRST_N)


def act_credit(e, g, s):
    e.sem_inc(s.x_hi, FIRST_N * 2)
    e.sem_inc(s.work_read, FIRST_N * g.items)
    e.sem_inc(s.q_sum, FIRST_N)
    e.sem_inc(s.exps, FIRST_N * 8)
    e.sem_inc(s.pt_hi, FIRST_N * 8)
    e.sem_inc(s.out_hi, FIRST_N * g.outs)


def dve_credit(e, g, s):
    e.sem_inc(s.x_lo, FIRST_N * 2)
    e.sem_inc(s.work_free, FIRST_N * g.items)
    e.sem_inc(s.newton, FIRST_N * 2 * NEWTON_OPS)
    e.sem_inc(s.row_max, FIRST_N * 8)
    e.sem_inc(s.neg_max, FIRST_N * 8)
    e.sem_inc(s.recip, FIRST_N * 8)
    e.sem_inc(s.pt_lo, FIRST_N * 8)
    e.sem_inc(s.out_lo, FIRST_N * g.outs)
    e.sem_inc(s.residual, FIRST_N)
    e.sem_inc(s.v_sum, FIRST_N * 4)


def pool_credit(e, g, s):
    e.sem_inc(s.rotated, FIRST_N * 8)
    e.sem_inc(s.k_scaled, FIRST_N * 4)
    e.sem_inc(s.probs, FIRST_N * 8)


def pe_item(e, g, s, b, item, c, nxt):
    kind, u = item
    j = g.index[item]
    bank = b.work[j % 3]
    base = c[g.items]
    e.wait_ge(s.work_free, base + j - 2)
    if kind == "PJ":
        isq, t, half = u // 4, (u % 4) // 2, u % 2
        col = (0 if isq else INNER) + 512 * half
        tok = slice(g.lead + P * t, g.lead + P * (t + 1))
        for k, (xp, wp) in enumerate([(b.xh, b.wh), (b.xh, b.wl), (b.xl, b.wh)]):
            mm = e.matmul(bank[:, :], xp[:, nxt, tok], wp[:, col:col + 512], start=(k == 0), stop=(k == 2))
    elif kind == "V":
        blk, half = divmod(u, 2)
        col = 2 * INNER + 512 * half
        tok = slice(BLOCK_Q * blk, BLOCK_Q * blk + BLOCK_K)
        for k, (xp, wp) in enumerate([(b.xh, b.wh), (b.xh, b.wl), (b.xl, b.wh)]):
            mm = e.matmul(bank[0:BLOCK_K, :], xp[:, nxt, tok], wp[:, col:col + 512], start=(k == 0), stop=(k == 2))
    elif kind in ("TQ", "TK"):
        if kind == "TQ":
            e.wait_ge(s.rotated, c[8] + 4 + u + 1)
            src = b.rot[:, 4 + u % 2, :]
        else:
            e.wait_ge(s.k_scaled, c[4] + u + 1)
            src = b.rot[:, u, :]
        for p in range(4):
            mm = e.transpose(bank[:, P * p:P * (p + 1)], src[:, P * p:P * (p + 1)], b.ident[:, :])
    elif kind in ("Q", "K"):
        col = 0 if kind == "Q" else DIM
        tok = slice(g.lead, g.lead + N_TOK)
        mm = bf16_parts_matmul(e, bank[:, 0:N_TOK], (b.wh[:, col:col + P], b.wl[:, col:col + P]),
                               (b.xh[:, nxt, tok], b.xl[:, nxt, tok]), True, True)
    else:
        tok = slice(BLOCK_Q * u, BLOCK_Q * u + BLOCK_K)
        mm = bf16_parts_matmul(e, bank[0:BLOCK_K, 0:DIM], (b.xh[:, nxt, tok], b.xl[:, nxt, tok]),
                               (b.wh[:, 2 * DIM:3 * DIM], b.wl[:, 2 * DIM:3 * DIM]), True, True)
    mm.then_inc(s.work_full, 1)


def pe_scores(e, g, s, b, m, c, par):
    t, row, rows, heads = quad_heads(g, m)
    bank = b.scores[m % 2]
    e.wait_ge(s.exps, c[8] + m - 1)
    if m == 0:
        e.wait_ge(s.work_free, c[g.items] + g.items)
    mask = b.maskb[:, b.mask_of(g, t), :].unsqueeze(1).broadcast_to([P, 4, BLOCK_K])
    e.matmul(bank[:, 0:4 * BLOCK_K].rearrange("p (h k) -> p h k", h=4), b.identb[:, :], mask,
             start=True, stop=False, skip_group_check=True)
    r = slice(row, row + rows)
    for k in range(2):
        blk = 2 * t + k
        for j, (slot, _) in enumerate(heads):
            qs = slice(P * t + BLOCK_Q * k, P * t + BLOCK_Q * (k + 1))
            ks = slice(BLOCK_Q * blk, BLOCK_Q * blk + BLOCK_K)
            kslot = 0 if g.first else slot
            last = bf16_parts_matmul(
                e, bank[64 * k:64 * k + 64, BLOCK_K * j:BLOCK_K * (j + 1)],
                (b.qh[r, par, slot, qs], b.ql[r, par, slot, qs]),
                (b.kh[r, par, kslot, ks], b.kl[r, par, kslot, ks]), False, (k == 1 and j == 3), skip=True)
    last.then_inc(s.scores, 1)


def pe_transpose_probs(e, g, s, b, m, c):
    e.wait_ge(s.probs, c[8] + m + 1)
    e.wait_ge(s.pt_lo, c[8] + m - 1)
    for j in range(4):
        mm = e.transpose(b.pt[m % 2][0:BLOCK_K, P * j:P * (j + 1)], b.probs[:, m % 2, j, :], b.ident[:, :])
    mm.then_inc(s.pt_full, 1)


def pe_values(e, g, s, b, m, c, par):
    t, row, rows, heads = quad_heads(g, m)
    e.wait_ge(s.pt_lo, c[8] + m + 1)
    if m % g.quads_per_out == 0:
        if m == 0:
            e.wait_ge(s.residual, c[1] + 0)
        else:
            e.wait_ge(s.out_lo, c[g.outs] + m // g.quads_per_out)
    for k in range(2):
        blk = 2 * t + k
        for j, (slot, h) in enumerate(heads):
            pts = slice(P * j + BLOCK_Q * k, P * j + BLOCK_Q * (k + 1))
            probs = (b.pth[:, m % 2, pts], b.ptl[:, m % 2, pts])
            if g.first:
                col = 128 * j + row
                v = (b.vmh[:, par, blk, col:col + 32], b.vml[:, par, blk, col:col + 32])
                out = b.out[row:row + 32, BLOCK_Q * k:BLOCK_Q * (k + 1)]
                mm = bf16_parts_matmul(e, out, v, probs, j == 0, j == 3)
            else:
                v = (b.vh[:, par, blk, DIM_HEAD * h:DIM_HEAD * (h + 1)], b.vl[:, par, blk, DIM_HEAD * h:DIM_HEAD * (h + 1)])
                col = P * (slot % 4) + BLOCK_Q * k
                out = b.out[row:row + 64, col:col + BLOCK_Q]
                mm = bf16_parts_matmul(e, out, v, probs, True, True)
    mm.then_inc(s.pv_full, 1)


def pe_project(e, g, s, b, c):
    e.wait_ge(s.out_lo, c[g.outs] + g.outs)
    for p in range(g.chunks):
        mm = bf16_parts_matmul(e, b.out[:, 0:N_TOK], (b.woh[:, p, :], b.wol[:, p, :]),
                               (b.oth[:, p, :], b.otl[:, p, :]), p == 0, p == g.chunks - 1)
    mm.then_inc(s.proj_full, 1)


def pe_slot(e, g, s, b, n, par, with_next):
    c = counts(e, n, (g.items, 8, 4, 2, g.outs, 1))
    cn = {per: v + per for per, v in c.items()}
    for m in range(STEPS):
        items = g.steps[m] if with_next else []
        if with_next and m == 0:
            e.wait_ge(s.x_lo, cn[2] + 2)
        if 1 <= m <= QUADS:
            pe_transpose_probs(e, g, s, b, m - 1, c)
        if m < QUADS:
            pe_scores(e, g, s, b, m, c, par)
        for item in items[:1]:
            pe_item(e, g, s, b, item, cn, 1 - par)
        if m >= 2:
            pe_values(e, g, s, b, m - 2, c, par)
        for item in items[1:]:
            pe_item(e, g, s, b, item, cn, 1 - par)
    pe_project(e, g, s, b, c)


def pe_first_items(e, g, s, b, n):
    c = counts(e, n, (g.items, 8, 4, 2))
    e.wait_ge(s.x_lo, c[2] + 2)
    for step in g.steps:
        for item in step:
            pe_item(e, g, s, b, item, c, 0)


def act_input(e, g, s, b, n, seq, par):
    c = counts(e, n, (g.items, 2))
    e.wait_ge(s.work_full, c[g.items] - g.items)
    if g.first:
        e.activation(b.xh[0:64, par, g.lead:g.lead + N_TOK], b.X[0:64, bass.ds(seq * N_TOK, N_TOK)], ACT.Copy).then_inc(s.x_hi, 1)
        e.activation(b.xh[64:P, par, g.lead:g.lead + N_TOK], b.X[64:P, bass.ds(seq * N_TOK, N_TOK)], ACT.Copy).then_inc(s.x_hi, 1)
    else:
        e.activation(b.xh[0:64, par, g.lead:PADDED], b.X[0:64, bass.ds(seq * N_TOK, N_TOK)], ACT.Copy).then_inc(s.x_hi, 1)
        e.activation(b.xh[64:P, par, g.lead + 1:PADDED], b.X[64:P, bass.ds(seq * N_TOK, N_TOK - 1)], ACT.Copy).then_inc(s.x_hi, 1)


def dve_input(e, g, s, b, n, seq, par):
    c = counts(e, n, (2,))
    skew = 0 if g.first else 1
    a = g.lead
    for k, (r, d) in enumerate([(slice(0, 64), 0), (slice(64, P), skew)]):
        e.wait_ge(s.x_hi, c[2] + k + 1)
        e.tensor_tensor(b.xl[r, par, a + d:a + N_TOK], b.X[r, bass.ds(seq * N_TOK, N_TOK - d)],
                        b.xh[r, par, a + d:a + N_TOK], ALU.subtract).then_inc(s.x_lo, 1)


def act_item(e, g, s, b, item, c, nxt):
    kind, u = item
    j = g.index[item]
    bank = b.work[j % 3]
    e.wait_ge(s.work_full, c[g.items] + j + 1)
    if kind == "PJ":
        if u >= 2:
            e.wait_ge(s.work_free, c[g.items] + g.index[("PJ", u - 2)] + 1)
        e.activation(b.sq[:, u % 2, :], bank[:, :], ACT.Square).then_inc(s.work_read, 1)
    elif kind == "V":
        blk, half = divmod(u, 2)
        e.activation(b.vh[:, nxt, blk, 512 * half:512 * (half + 1)], bank[0:BLOCK_K, :], ACT.Copy).then_inc(s.work_read, 1)
    elif kind in ("TQ", "TK"):
        t, half = divmod(u, 2)
        dst, off = (b.qh, 0) if kind == "TQ" else (b.kh, g.lead)
        e.activation(dst[:, nxt, 4 * half:4 * half + 4, off + P * t:off + P * (t + 1)],
                     bank[:, :].rearrange("p (h t) -> p h t", h=4), ACT.Copy).then_inc(s.work_read, 1)
    elif kind == "Q":
        e.activation(b.q0[:, :], bank[:, 0:N_TOK], ACT.Identity, bias=b.qkb[:, 0:1]).then_inc(s.q_sum, 1)
        e.wait_ge(s.q_sum, c[1] + 1)
        for r in range(4):
            op = e.activation(b.qh[:, nxt, r, :], b.q0[:, :], ACT.Copy, scale=b.rowmask[:, r:r + 1])
        op.then_inc(s.work_read, 1)
    elif kind == "K":
        e.activation(b.kh[:, nxt, 0, g.lead:g.lead + N_TOK], bank[:, 0:N_TOK], ACT.Identity, bias=b.qkb[:, 1:2]).then_inc(s.work_read, 1)
    else:
        e.wait_ge(s.v_sum, c[4] + u + 1)
        e.activation(first_values(b.vmh, nxt, u), b.v0[:, :].rearrange("p (g r d) -> p r g d", g=4, r=4), ACT.Copy).then_inc(s.work_read, 1)


def first_values(v, par, blk):
    flat = v[:, par, blk, :].rearrange("p (r x) -> p r x", r=4)
    return flat[:, :, 0:128].rearrange("p r (g y) -> p r g y", g=4)[:, :, :, 0:HEAD_DIM0]


def act_exp(e, g, s, b, m, c, par):
    t, row, rows, heads = quad_heads(g, m)
    if m == 0 and not g.first:
        e.wait_ge(s.newton, c[2 * NEWTON_OPS] + 2 * NEWTON_OPS)
    e.wait_ge(s.neg_max, c[8] + m + 1)
    e.wait_ge(s.pt_full, c[8] + m - 1)
    for j, (_, h) in enumerate(heads):
        scale = SCALE0 if g.first else b.rq[:, par, t * HEADS + h:t * HEADS + h + 1]
        op = e.activation(b.probs[:, m % 2, j, :], b.scores[m % 2][:, BLOCK_K * j:BLOCK_K * (j + 1)], ACT.Exp,
                          bias=b.nmax[:, m % 2, j:j + 1], scale=scale, accum_out=b.den[:, m % 2, j:j + 1])
    op.then_inc(s.exps, 1)


def act_probs_hi(e, g, s, b, m, c):
    e.wait_ge(s.pt_full, c[8] + m + 1)
    e.wait_ge(s.pv_full, c[8] + m - 1)
    e.activation(b.pth[:, m % 2, :], b.pt[m % 2][0:BLOCK_K, :], ACT.Copy).then_inc(s.pt_hi, 1)


def out_views(g, b, i, part):
    if g.first:
        return part[:, 0, P * i:P * (i + 1)], b.out[:, 0:P]
    t, half = divmod(i, 2)
    return (part[:, 4 * half:4 * half + 4, P * t:P * (t + 1)],
            b.out[:, :].rearrange("p (h t) -> p h t", h=4))


def act_out_hi(e, g, s, b, i, c):
    e.wait_ge(s.pv_full, c[8] + g.quads_per_out * (i + 1))
    if i == 0:
        e.wait_ge(s.proj_full, c[1] + 0)
    dst, src = out_views(g, b, i, b.oth)
    e.activation(dst, src, ACT.Copy).then_inc(s.out_hi, 1)


def act_slot(e, g, s, b, n, seq, par, with_next, with_input):
    c = counts(e, n, (g.items, 8, 4, 2, g.outs, 1, 2 * NEWTON_OPS))
    cn = {per: v + per for per, v in c.items()}
    for m in range(STEPS):
        items = g.steps[m] if with_next else []
        if 1 <= m <= QUADS:
            act_probs_hi(e, g, s, b, m - 1, c)
        if m < QUADS:
            act_exp(e, g, s, b, m, c, par)
        for item in items[:1]:
            act_item(e, g, s, b, item, cn, 1 - par)
        if m >= 2 and (m - 1) % g.quads_per_out == 0:
            act_out_hi(e, g, s, b, (m - 1) // g.quads_per_out - 1, c)
        for item in items[1:]:
            act_item(e, g, s, b, item, cn, 1 - par)
    if with_input:
        act_input(e, g, s, b, n + 2, seq + 2, par)


def act_first_items(e, g, s, b, n, seq):
    act_input(e, g, s, b, n, seq, 0)
    act_input(e, g, s, b, n + 1, seq + 1, 1)
    c = counts(e, n, (g.items, 4, 1))
    for step in g.steps:
        for item in step:
            act_item(e, g, s, b, item, c, 0)


def dve_item(e, g, s, b, item, c, nxt):
    kind, u = item
    j = g.index[item]
    bank = b.work[j % 3]
    if kind == "V0":
        e.wait_ge(s.work_full, c[g.items] + j + 1)
        if u > 0:
            e.wait_ge(s.work_free, c[g.items] + j)
        e.tensor_tensor(b.v0[:, :], bank[0:BLOCK_K, 0:DIM], b.vbias[:, :], ALU.add).then_inc(s.v_sum, 1)
    e.wait_ge(s.work_read, c[g.items] + j + 1)
    if kind == "PJ":
        isq, t, half = u // 4, (u % 4) // 2, u % 2
        col = (0 if isq else 2 * HEADS) + HEADS * t + 8 * half
        e.tensor_reduce(b.ss[:, nxt, col:col + 8], b.sq[:, u % 2, :].rearrange("p (h d) -> p h d", h=8), AX_X, ALU.add)
        pj = bank[:, :].rearrange("p (h s d) -> p h s d", h=8, s=2)
        first = 0 if isq else 2
        cos = b.table[:, t, first, :].rearrange("p (s d) -> p s d", s=2).unsqueeze(1).broadcast_to([P, 8, 2, 32])
        sin = b.table[:, t, first + 1, :].rearrange("p (s d) -> p s d", s=2).unsqueeze(1).broadcast_to([P, 8, 2, 32])
        e.wait_ge(s.rotated, c[8] + u - 1)
        e.tensor_tensor(b.m1[:, u % 2, :].rearrange("p (h s d) -> p h s d", h=8, s=2), pj, cos, ALU.mult)
        e.tensor_tensor(b.m2[:, u % 2, :].rearrange("p (h s d) -> p h s d", h=8, s=2), pj[:, :, ::-1, :], sin,
                        ALU.mult).then_inc(s.work_free, 1)
    elif kind == "V":
        blk, half = divmod(u, 2)
        v = slice(512 * half, 512 * (half + 1))
        e.tensor_tensor(b.vl[:, nxt, blk, v], bank[0:BLOCK_K, :], b.vh[:, nxt, blk, v], ALU.subtract).then_inc(s.work_free, 1)
    elif kind in ("TQ", "TK"):
        t, half = divmod(u, 2)
        hi, lo, off = (b.qh, b.ql, 0) if kind == "TQ" else (b.kh, b.kl, g.lead)
        where = (slice(None), nxt, slice(4 * half, 4 * half + 4), slice(off + P * t, off + P * (t + 1)))
        e.tensor_tensor(lo[where], bank[:, :].rearrange("p (h t) -> p h t", h=4), hi[where],
                        ALU.subtract).then_inc(s.work_free, 1)
    elif kind == "Q":
        for r in range(4):
            op = e.scalar_tensor_tensor(b.ql[:, nxt, r, :], b.q0[:, :], b.rowmask[:, r:r + 1], b.qh[:, nxt, r, :],
                                        ALU.mult, ALU.subtract)
        op.then_inc(s.work_free, 1)
    elif kind == "K":
        k = slice(g.lead, g.lead + N_TOK)
        e.scalar_tensor_tensor(b.kl[:, nxt, 0, k], bank[:, 0:N_TOK], b.qkb[:, 1:2], b.kh[:, nxt, 0, k],
                               ALU.add, ALU.subtract).then_inc(s.work_free, 1)
    else:
        e.tensor_tensor(first_values(b.vml, nxt, u), b.v0[:, :].rearrange("p (g r d) -> p r g d", g=4, r=4),
                        first_values(b.vmh, nxt, u), ALU.subtract).then_inc(s.work_free, 1)


def dve_newton(e, g, s, b, i, c, nxt):
    isq, op = divmod(i, NEWTON_OPS)
    cols = slice(0, 2 * HEADS) if isq else slice(2 * HEADS, 4 * HEADS)
    if op == 0:
        last = g.index[("PJ", 7 if isq else 3)]
        e.wait_ge(s.work_free, c[g.items] + last + 1)
    e.wait_ge(s.newton, c[2 * NEWTON_OPS] + i)
    x, a = b.nx[:, cols], b.na[:, cols]
    y = b.rq[:, nxt, :] if isq else b.rk[:, :]
    scale = 1.0 / (QK_SCALE * QK_SCALE) if isq else 1.0
    rsqrt_op(e, op, x, y, a, b.ss[:, nxt, cols], 1e-24, scale).then_inc(s.newton, 1)


def dve_max(e, g, s, b, m, c, par):
    t, row, rows, heads = quad_heads(g, m)
    e.wait_ge(s.scores, c[8] + m + 1)
    e.tensor_reduce(b.rmax[:, m % 2, :], b.scores[m % 2][:, 0:4 * BLOCK_K].rearrange("p (h k) -> p h k", h=4),
                    AX_X, ALU.max).then_inc(s.row_max, 1)
    e.wait_ge(s.row_max, c[8] + m + 1)
    if g.first:
        e.tensor_scalar(b.nmax[:, m % 2, :], b.rmax[:, m % 2, :], -SCALE0, None, ALU.mult).then_inc(s.neg_max, 1)
    else:
        h0 = t * HEADS + heads[0][1]
        e.scalar_tensor_tensor(b.nmax[:, m % 2, :], b.rmax[:, m % 2, :], -1.0, b.rq[:, par, h0:h0 + 7:2],
                               ALU.mult, ALU.mult).then_inc(s.neg_max, 1)


def dve_recip(e, g, s, b, m, c):
    e.wait_ge(s.exps, c[8] + m + 1)
    e.reciprocal(b.rden[:, m % 2, :], b.den[:, m % 2, :]).then_inc(s.recip, 1)


def dve_probs_lo(e, g, s, b, m, c):
    e.wait_ge(s.pt_hi, c[8] + m + 1)
    e.tensor_tensor(b.ptl[:, m % 2, :], b.pt[m % 2][0:BLOCK_K, :], b.pth[:, m % 2, :], ALU.subtract).then_inc(s.pt_lo, 1)


def dve_out_lo(e, g, s, b, i, c):
    e.wait_ge(s.out_hi, c[g.outs] + i + 1)
    dst, src = out_views(g, b, i, b.otl)
    hi, _ = out_views(g, b, i, b.oth)
    e.tensor_tensor(dst, src, hi, ALU.subtract).then_inc(s.out_lo, 1)


def dve_residual(e, g, s, b, c, seq):
    e.wait_ge(s.proj_full, c[1] + 1)
    if g.first:
        x = b.X1[:, bass.ds(seq * N_TOK, N_TOK)]
        e.scalar_tensor_tensor(x, b.out[:, 0:N_TOK], b.qkb[:, 2:3], x, ALU.add, ALU.add).then_inc(s.residual, 1)
    else:
        x = b.X[:, bass.ds(seq * N_TOK, N_TOK)]
        e.tensor_tensor(x, b.out[:, 0:N_TOK], x, ALU.add).then_inc(s.residual, 1)


NEWTON_AT = {2: range(0, 4), 3: range(4, 8), 4: range(8, 11), 6: range(11, 15), 7: range(15, 19), 8: range(19, 22)}


def dve_slot(e, g, s, b, n, seq, par, with_next, with_input):
    c = counts(e, n, (g.items, 8, 4, 2, g.outs, 1, 2 * NEWTON_OPS))
    cn = {per: v + per for per, v in c.items()}
    for m in range(STEPS):
        items = g.steps[m] if with_next else []
        newton = list(NEWTON_AT.get(m, ())) if with_next and not g.first else []

        def step_newton():
            if newton:
                dve_newton(e, g, s, b, newton.pop(0), cn, 1 - par)

        if 1 <= m <= QUADS:
            dve_probs_lo(e, g, s, b, m - 1, c)
        step_newton()
        if m < QUADS:
            dve_max(e, g, s, b, m, c, par)
        step_newton()
        for item in items[:1]:
            dve_item(e, g, s, b, item, cn, 1 - par)
        step_newton()
        if m < QUADS:
            dve_recip(e, g, s, b, m, c)
        if m >= 2 and (m - 1) % g.quads_per_out == 0:
            dve_out_lo(e, g, s, b, (m - 1) // g.quads_per_out - 1, c)
        step_newton()
        for item in items[1:]:
            dve_item(e, g, s, b, item, cn, 1 - par)
        while newton:
            step_newton()
    dve_residual(e, g, s, b, c, seq)
    if with_input:
        dve_input(e, g, s, b, n + 2, seq + 2, par)


def dve_first_items(e, g, s, b, n, seq):
    dve_input(e, g, s, b, n, seq, 0)
    dve_input(e, g, s, b, n + 1, seq + 1, 1)
    c = counts(e, n, (g.items, 8, 4, 2 * NEWTON_OPS))
    for m, step in enumerate(g.steps):
        for item in step:
            dve_item(e, g, s, b, item, c, 0)
        if not g.first:
            for i in NEWTON_AT.get(m, ()):
                dve_newton(e, g, s, b, i, c, 0)


def pool_rotate(e, g, s, b, u, c):
    e.wait_ge(s.work_free, c[g.items] + g.index[("PJ", u)] + 1)
    if u < 4:
        e.wait_ge(s.work_full, c[g.items] + g.index[("TK", u)] + 1 - g.items)
        slot = u
    else:
        i = g.index[("TQ", u - 6)] if u >= 6 else g.index[("TQ", u - 2)] - g.items
        e.wait_ge(s.work_full, c[g.items] + i + 1)
        slot = 4 + u % 2
    e.tensor_tensor(b.rot[:, slot, :], b.m1[:, u % 2, :], b.m2[:, u % 2, :], ALU.add).then_inc(s.rotated, 1)


def pool_scale_k(e, g, s, b, u, c):
    if u == 0:
        e.wait_ge(s.newton, c[2 * NEWTON_OPS] + NEWTON_OPS)
        e.wait_ge(s.rotated, c[8] + 4)
    t, half = divmod(u, 2)
    rk = b.rk[:, t * HEADS + 8 * half:t * HEADS + 8 * half + 8].unsqueeze(2).broadcast_to([P, 8, DIM_HEAD])
    v = b.rot[:, u, :].rearrange("p (h d) -> p h d", h=8)
    e.tensor_tensor(v, v, rk, ALU.mult).then_inc(s.k_scaled, 1)


def pool_normalise(e, g, s, b, m, c):
    e.wait_ge(s.recip, c[8] + m + 1)
    p = b.probs[:, m % 2, :, :]
    e.tensor_tensor(p, p, b.rden[:, m % 2, :].unsqueeze(2).broadcast_to([P, 4, BLOCK_K]), ALU.mult).then_inc(s.probs, 1)


SCALE_K_AT = {5: (0, 1), 6: (2, 3)}


def pool_items(e, g, s, b, m, c):
    if g.first:
        return
    for u in SCALE_K_AT.get(m, ()):
        pool_scale_k(e, g, s, b, u, c)
    for kind, u in g.steps[m]:
        if kind == "PJ":
            pool_rotate(e, g, s, b, u, c)


def pool_slot(e, g, s, b, n, with_next):
    c = counts(e, n, (g.items, 8, 4, 2 * NEWTON_OPS))
    cn = {per: v + per for per, v in c.items()}
    for m in range(STEPS):
        if m < QUADS:
            pool_normalise(e, g, s, b, m, c)
        if with_next:
            pool_items(e, g, s, b, m, cn)


def pool_first_items(e, g, s, b, n):
    c = counts(e, n, (g.items, 8, 4, 2 * NEWTON_OPS))
    for m in range(STEPS):
        pool_items(e, g, s, b, m, c)


def sequences(e, first_n, slot, head):
    head(first_n)
    with e.Fori(0, 7) as i:
        for par in range(2):
            seq = e.snap(i * 2 + par)
            slot(e.snap(first_n + seq), seq, par, True, True)
    slot(first_n + 14, 14, 0, True, False)
    slot(first_n + 15, 15, 1, False, False)


def attention_programs(g, s, b):
    def pe(e, n):
        sequences(e, n, lambda n, seq, par, nxt, inp: pe_slot(e, g, s, b, n, par, nxt),
                  lambda n: pe_first_items(e, g, s, b, n))

    def act(e, n):
        sequences(e, n, lambda n, seq, par, nxt, inp: act_slot(e, g, s, b, n, seq, par, nxt, inp),
                  lambda n: act_first_items(e, g, s, b, n, 0))

    def dve(e, n):
        sequences(e, n, lambda n, seq, par, nxt, inp: dve_slot(e, g, s, b, n, seq, par, nxt, inp),
                  lambda n: dve_first_items(e, g, s, b, n, 0))

    def pool(e, n):
        sequences(e, n, lambda n, seq, par, nxt, inp: pool_slot(e, g, s, b, n, nxt),
                  lambda n: pool_first_items(e, g, s, b, n))

    return pe, act, dve, pool



class FfnSems:

    def __init__(self, ctx, nc, tag):
        def sem(name):
            return ctx.enter_context(nc.semaphore(f"{tag}_{name}"))

        self.shifted = sem("shifted")
        self.mean = sem("mean")
        self.centred = sem("centred")
        self.squares = sem("squares")
        self.variance = sem("variance")
        self.newton = sem("newton")
        self.diag = sem("diag")
        self.rstd = sem("rstd")
        self.normed = sem("normed")
        self.affine = sem("affine")
        self.n_hi = sem("n_hi")
        self.n_lo = sem("n_lo")
        self.up_full = sem("up_full")
        self.gelu = sem("gelu")
        self.gated = sem("gated")
        self.g_hi = sem("g_hi")
        self.g_lo = sem("g_lo")
        self.down_full = sem("down_full")
        self.residual = sem("residual")


def pe_ffn_credit(e, s):
    e.sem_inc(s.mean, UNITS)
    e.sem_inc(s.variance, UNITS)
    e.sem_inc(s.rstd, UNITS)
    e.sem_inc(s.up_full, NF * UNITS)
    e.sem_inc(s.down_full, UNITS)


def act_ffn_credit(e, s):
    e.sem_inc(s.shifted, UNITS)
    e.sem_inc(s.affine, UNITS)
    e.sem_inc(s.gelu, NF * UNITS)


def dve_ffn_credit(e, s):
    e.sem_inc(s.centred, UNITS)
    e.sem_inc(s.newton, NEWTON_OPS + 1)
    e.sem_inc(s.diag, UNITS)
    e.sem_inc(s.normed, UNITS)
    e.sem_inc(s.n_hi, UNITS)
    e.sem_inc(s.gated, NF * UNITS)
    e.sem_inc(s.g_hi, NF * UNITS)
    e.sem_inc(s.residual, UNITS)


def pool_ffn_credit(e, s):
    e.sem_inc(s.squares, UNITS)
    e.sem_inc(s.n_lo, UNITS)
    e.sem_inc(s.g_lo, NF * UNITS)


def unit(a, u):
    return a[:, bass.ds(u * UNIT, UNIT)]


def norm_source(b, plain, u):
    return unit(b.X1, u) if plain else b.xs[:, u % 2, :]


def stats_act(e, s, b, layer):
    base = layer * UNITS + UNITS
    for u in range(UNITS):
        e.wait_ge(s.centred, base + u - 1)
        e.activation(b.xs[0:64, u % 2, :], b.X[0:64, u * UNIT:(u + 1) * UNIT], ACT.Copy)
        dst = b.xs[64:P, u % 2, :].rearrange("p (q t) -> p q t", t=N_TOK)
        src = b.X[64:P, u * UNIT:(u + 1) * UNIT].rearrange("p (q t) -> p q t", t=N_TOK)
        e.activation(dst[:, :, 1:N_TOK], src[:, :, 0:N_TOK - 1], ACT.Copy).then_inc(s.shifted, 1)


def stats_pe(e, s, b, base, plain):
    for u in range(UNITS + 1):
        if u < UNITS:
            if not plain:
                e.wait_ge(s.shifted, base + u + 1)
            e.wait_ge(s.centred, base + u - 1)
            e.matmul(b.bank[u % 2][:, :], b.inv_dim[:, :], norm_source(b, plain, u), start=True, stop=True).then_inc(s.mean, 1)
        if u >= 1:
            e.wait_ge(s.squares, base + u)
            for t in range(4):
                v = 4 * (u - 1) + t
                mm = e.matmul(b.bank[2][:, v:v + 1], b.sqc[:, (u - 1) % 2, P * t:P * (t + 1)], b.inv_dim[:, 0:1],
                              start=True, stop=True)
            mm.then_inc(s.variance, 1)


def stats_dve(e, s, b, base, plain):
    for u in range(UNITS):
        e.wait_ge(s.mean, base + u + 1)
        if u == 0:
            e.wait_ge(s.normed, base + 0)
        e.tensor_tensor(unit(b.xc, u), norm_source(b, plain, u), b.bank[u % 2][:, :], ALU.subtract).then_inc(s.centred, 1)


def stats_pool(e, s, b, base):
    for u in range(UNITS):
        e.wait_ge(s.centred, base + u + 1)
        e.wait_ge(s.variance, base + u - 1)
        e.tensor_tensor(b.sqc[:, u % 2, :], unit(b.xc, u), unit(b.xc, u), ALU.mult).then_inc(s.squares, 1)


def rstd_dve(e, s, b, base, base_newton):
    e.wait_ge(s.variance, base + UNITS)
    e.tensor_scalar(b.var[:, :], b.bank[2][:, 0:4 * UNITS], LN_EPS, None, ALU.add).then_inc(s.newton, 1)
    for i in range(NEWTON_OPS):
        e.wait_ge(s.newton, base_newton + i + 1)
        rsqrt_op(e, i, b.nx[:, 0:32], b.rstd[:, :], b.na[:, 0:32], b.var[:, :], 0.0, 1.0).then_inc(s.newton, 1)


def norm_dve_diag(e, s, b, base, base_newton, u, par):
    e.wait_ge(s.newton, base_newton + NEWTON_OPS + 1)
    e.wait_ge(s.rstd, base - 1)
    e.tensor_tensor(b.diag[:, par, :, :], b.ident[:, :].unsqueeze(1).broadcast_to([P, 4, P]),
                    b.rstd[:, bass.ds(u * 4, 4)].unsqueeze(2).broadcast_to([P, 4, P]), ALU.mult).then_inc(s.diag, 1)


def norm_pe(e, s, b, base, par):
    e.wait_ge(s.diag, base + 1)
    e.wait_ge(s.normed, base + 0)
    e.matmul(b.bank[0][:, :], b.ones[:, :], b.diag[:, par, :, :].rearrange("p a b -> p (a b)"), start=True, stop=True).then_inc(s.rstd, 1)


def norm_dve(e, s, b, base, u, dst):
    e.wait_ge(s.rstd, base + 1)
    e.tensor_tensor(unit(dst, u), unit(b.xc, u), b.bank[0][:, :], ALU.mult).then_inc(s.normed, 1)


def affine_act(e, s, b, base, u, par):
    e.wait_ge(s.normed, base + 1)
    e.wait_ge(s.n_lo, base - 1)
    e.activation(b.xn[:, par, :], unit(b.xc, u), ACT.Identity, bias=b.vec[:, 1:2], scale=b.vec[:, 0:1]).then_inc(s.affine, 1)


def affine_dve_hi(e, s, b, base, base3, par):
    e.wait_ge(s.affine, base + 1)
    e.wait_ge(s.up_full, base3 - NF)
    e.tensor_copy(b.xnh[:, par, :], b.xn[:, par, :]).then_inc(s.n_hi, 1)


def affine_pool_lo(e, s, b, base, par):
    e.wait_ge(s.n_hi, base + 1)
    e.tensor_tensor(b.xnl[:, par, :], b.xn[:, par, :], b.xnh[:, par, :], ALU.subtract).then_inc(s.n_lo, 1)


def up_pe(e, s, b, base, base3, par):
    e.wait_ge(s.n_lo, base + 1)
    for c, (at, size) in enumerate(F_CHUNKS):
        ring = (par + c) % 2
        e.wait_ge(s.gated, base3 + c - 1)
        for k, off in enumerate((DIM_INNER, 0)):
            w = slice(off + at, off + at + size)
            mm = bf16_parts_matmul(e, b.bank[1 + 2 * ring + k][0:size, :], (b.w1h[:, w], b.w1l[:, w]),
                                   (b.xnh[:, par, :], b.xnl[:, par, :]), True, True)
        mm.then_inc(s.up_full, 1)


def gelu_act(e, s, b, base3, par):
    for c, (at, size) in enumerate(F_CHUNKS):
        ring = (par + c) % 2
        e.wait_ge(s.up_full, base3 + c + 1)
        e.wait_ge(s.gated, base3 + c - 1)
        e.activation(b.ge[0:size, ring, :], b.bank[1 + 2 * ring][0:size, :], ACT.Gelu,
                     bias=b.vec[0:size, 5 + c:6 + c]).then_inc(s.gelu, 1)


def gate_dve(e, s, b, base, base3, par):
    for c, (at, size) in enumerate(F_CHUNKS):
        ring = (par + c) % 2
        e.wait_ge(s.gelu, base3 + c + 1)
        e.wait_ge(s.g_lo, base3 + c - 1)
        e.scalar_tensor_tensor(b.hf[0:size, ring, :], b.bank[2 + 2 * ring][0:size, :], b.vec[0:size, 2 + c:3 + c],
                               b.ge[0:size, ring, :], ALU.add, ALU.mult).then_inc(s.gated, 1)
        e.wait_ge(s.gated, base3 + c + 1)
        if c == 0:
            e.wait_ge(s.down_full, base - 1)
        e.tensor_copy(b.hh[0:size, par, c, :], b.hf[0:size, ring, :]).then_inc(s.g_hi, 1)


def gate_pool_lo(e, s, b, base3, par):
    for c, (at, size) in enumerate(F_CHUNKS):
        ring = (par + c) % 2
        e.wait_ge(s.g_hi, base3 + c + 1)
        e.tensor_tensor(b.hl[0:size, par, c, :], b.hf[0:size, ring, :], b.hh[0:size, par, c, :], ALU.subtract).then_inc(s.g_lo, 1)


def down_pe(e, s, b, base, base3, par):
    e.wait_ge(s.g_lo, base3 + NF)
    e.wait_ge(s.residual, base - 1)
    for c, (at, size) in enumerate(F_CHUNKS):
        mm = bf16_parts_matmul(e, b.bank[5 + par][:, :], (b.w2h[0:size, c, :], b.w2l[0:size, c, :]),
                               (b.hh[0:size, par, c, :], b.hl[0:size, par, c, :]), c == 0, c == NF - 1)
    mm.then_inc(s.down_full, 1)


def down_dve(e, s, b, base, u, par):
    e.wait_ge(s.down_full, base + 1)
    x = unit(b.X, u)
    e.scalar_tensor_tensor(x, b.bank[5 + par][:, :], b.vec[:, 8:9], x, ALU.add, ALU.add).then_inc(s.residual, 1)


def ffn_units(e, base, norm, up, down):
    def at(u):
        return e.snap(base + u), e.snap(base * NF + u * NF)

    def ahead(u, par):
        norm(*at(u), u, par)

    ahead(0, 0)
    ahead(1, 1)
    up(*at(0), 0, 0)
    with e.Fori(0, (UNITS - 2) // 2) as i:
        for k in range(2):
            u = e.snap(i * 2 + k + 1)
            ahead(e.snap(u + 1), k)
            up(*at(u), u, 1 - k)
            down(*at(e.snap(u - 1)), e.snap(u - 1), k)
    up(*at(UNITS - 1), UNITS - 1, 1)
    down(*at(UNITS - 2), UNITS - 2, 0)
    down(*at(UNITS - 1), UNITS - 1, 1)



def build(nc, x_t, w0, wo0, vec0, vbias, masks, ident, inv_dim, ones, rope, rowmask, wqkv, qks, wo, w1, w2, vecs, out_t):
    with ExitStack() as ctx:
        def sb(name, shape, dt=F32):
            return ctx.enter_context(nc.sbuf_tensor(name, shape, dt))

        def sem(name):
            return ctx.enter_context(nc.semaphore(name))

        b = Buffers()
        b.bank = [ctx.enter_context(nc.psum_tensor(f"bank{i}", [P, 512], F32)) for i in range(8)]
        b.work, b.scores, b.pt, b.out = b.bank[0:3], b.bank[3:5], b.bank[5:7], b.bank[7]

        b.X = sb("x_stream", [P, TOKENS])
        b.X1 = sb("x_outer", [P, TOKENS])
        W_ATT = 3 * INNER + INNER
        W_FFN = 2 * DIM_INNER + NF * DIM
        watt_f = sb("watt_f32", [P, W_ATT])
        wffn_f = sb("wffn_f32", [P, W_FFN])
        watt = [sb(f"watt_{k}", [P, W_ATT], BF16) for k in ("hi", "lo")]
        wffn = [sb(f"wffn_{k}", [P, W_FFN], BF16) for k in ("hi", "lo")]
        b.wh, b.wl = (w[:, 0:3 * INNER] for w in watt)
        b.woh, b.wol = (w[:, 3 * INNER:].rearrange("p (c d) -> p c d", c=INNER // P) for w in watt)
        b.w1h, b.w1l = (w[:, 0:2 * DIM_INNER] for w in wffn)
        b.w2h, b.w2l = (w[:, 2 * DIM_INNER:].rearrange("p (c d) -> p c d", c=NF) for w in wffn)

        b.ident, b.inv_dim, b.ones = sb("ident", [P, P]), sb("inv_dim", [P, P]), sb("ones", [P, P])
        b.identb = sb("identb", [P, P], BF16)
        maskf = sb("maskf", [P, 5, BLOCK_K])
        b.maskb = sb("maskb", [P, 5, BLOCK_K], BF16)
        b.mask_of = lambda g, t: t if g.first else 2 + t
        rope_sb = sb("rope", [P, 2, 4, DIM_HEAD])
        qks_sb = sb("qks", [P, 4, DIM_HEAD])
        b.table = sb("table", [P, 2, 4, DIM_HEAD])
        b.rowmask = sb("rowmask", [P, 4])
        b.qkb = sb("bias0", [P, 3])
        b.vbias = sb("vbias0", [BLOCK_K, DIM])
        vecs_sb = sb("vecs", [P, DEPTH, 9])
        b.vec = sb("vec", [P, 9])

        qbuf = sb("qbuf", [P, 2 * 2 * 8 * N_TOK // 2])
        kbuf = sb("kbuf", [P, 2 * 2 * 8 * PADDED], BF16)
        vbuf = sb("vbuf", [P, 2 * 2 * BLOCKS * INNER // 2])
        q4 = qbuf[:, :].bitcast(BF16).rearrange("p (h a s t) -> p h a s t", h=2, a=2, s=8)
        b.qh, b.ql = q4[:, 0], q4[:, 1]
        k4 = kbuf[:, :].rearrange("p (h a s t) -> p h a s t", h=2, a=2, s=8)
        b.kh, b.kl = k4[:, 0], k4[:, 1]
        v4 = vbuf[0:BLOCK_K, :].bitcast(BF16).rearrange("p (h a s t) -> p h a s t", h=2, a=2, s=BLOCKS)
        b.vh, b.vl = v4[:, 0], v4[:, 1]
        VM = 544
        b.vmh, b.vml = v4[:, 0, :, :, 0:VM], v4[:, 1, :, :, 0:VM]

        rotbuf = sb("rotbuf", [P, 6 * 512])
        b.rot = rotbuf[:, :].rearrange("p (s d) -> p s d", s=6)
        mbuf = sb("mbuf", [P, 4 * 512])
        m4 = mbuf[:, :].rearrange("p (k s d) -> p k s d", k=2, s=2)
        b.m1, b.m2 = m4[:, 0], m4[:, 1]
        b.q0 = mbuf[:, 0:N_TOK]
        b.v0 = mbuf[0:BLOCK_K, 512:512 + DIM]
        b.sq = sb("sq", [P, 2, 512])
        b.ss = sb("ss", [P, 2, 4 * HEADS])
        b.nx, b.na = sb("newton_x", [P, 4 * HEADS]), sb("newton_a", [P, 4 * HEADS])
        b.rk, b.rq = sb("rk", [P, 2 * HEADS]), sb("rq", [P, 2, 2 * HEADS])
        b.rmax, b.nmax = sb("rmax", [P, 2, 4]), sb("nmax", [P, 2, 4])
        b.den, b.rden = sb("den", [P, 2, 4]), sb("rden", [P, 2, 4])
        b.probs = sb("probs", [P, 2, 4, BLOCK_K])
        b.pth, b.ptl = sb("pth", [BLOCK_K, 2, 512], BF16), sb("ptl", [BLOCK_K, 2, 512], BF16)
        b.oth, b.otl = sb("oth", [P, 8, N_TOK], BF16), sb("otl", [P, 8, N_TOK], BF16)
        b.xh, b.xl = sb("xh", [P, 2, PADDED], BF16), sb("xl", [P, 2, PADDED], BF16)

        def pair(a, at, n=2):
            return a[:, at:at + n * UNIT].rearrange("p (s t) -> p s t", s=n)

        b.xc = vbuf[:, 0:TOKENS]
        b.xn = pair(vbuf, TOKENS)
        b.xnh, b.xnl = (vbuf[:, TOKENS + 2 * UNIT + UNIT * k:TOKENS + 2 * UNIT + UNIT * (k + 1)].bitcast(BF16)
                        .rearrange("p (s t) -> p s t", s=2) for k in range(2))
        b.xs = pair(qbuf, 0)
        b.sqc = pair(qbuf, 2 * UNIT)
        b.ge = pair(qbuf, 2 * UNIT)
        b.hf = pair(mbuf, 0)
        b.diag = pair(mbuf, 2 * UNIT).rearrange("p s (a t) -> p s a t", a=4)
        b.hh, b.hl = (rotbuf[:, 3 * UNIT * k:3 * UNIT * (k + 1)].bitcast(BF16).rearrange("p (s c t) -> p s c t", s=2, c=NF)
                      for k in range(2))
        b.var, b.rstd = sb("var", [P, 4 * UNITS]), sb("rstd", [P, 4 * UNITS])

        g0, g1 = Geometry(True), Geometry(False)

        loaded, const_ready = sem("loaded"), sem("const_ready")
        loads = [(b.X1[:, :], x_t), (b.ident[:, :], ident), (b.inv_dim[:, :], inv_dim), (b.ones[:, :], ones),
                 (maskf[:, :, :], masks), (rope_sb[:, :, :, :], rope), (b.rowmask[:, :], rowmask), (b.qkb[:, :], vec0),
                 (b.vbias[:, :], vbias), (vecs_sb[:, :, :], vecs), (watt_f[:, 0:3 * DIM], w0),
                 (watt_f[:, 3 * INNER:3 * INNER + DIM], wo0)]
        with nc.Block() as block:
            @block.sync
            def _(sp):
                for dst, src in loads:
                    sp.dma_start(dst, src).then_inc(loaded, 16)

            @block.gpsimd
            def _(pool):
                pool.memset(kbuf[:, :], 0.0)
                pool.memset(b.xh[:, :, :], 0.0)
                pool.memset(b.xl[:, :, :], 0.0)

            @block.vector
            def _(dve):
                dve.memset(vbuf[:, :], 0.0)
                dve.wait_ge(loaded, 16 * len(loads))
                dve.tensor_copy(b.identb[:, :], b.ident[:, :])
                dve.tensor_copy(b.maskb[:, :, :], maskf[:, :, :])
                dve.wait_ge(const_ready, 2)
                dve.tensor_tensor(b.wl[:, 0:3 * DIM], watt_f[:, 0:3 * DIM], b.wh[:, 0:3 * DIM], ALU.subtract)
                dve.tensor_tensor(b.wol[:, 0, :], watt_f[:, 3 * INNER:3 * INNER + DIM], b.woh[:, 0, :], ALU.subtract)

            @block.scalar
            def _(act):
                act.wait_ge(loaded, 16 * len(loads))
                act.activation(b.wh[:, 0:3 * DIM], watt_f[:, 0:3 * DIM], ACT.Copy).then_inc(const_ready, 1)
                act.activation(b.woh[:, 0, :], watt_f[:, 3 * INNER:3 * INNER + DIM], ACT.Copy).then_inc(const_ready, 1)

        def layer_norm(tag):
            s = FfnSems(ctx, nc, tag)
            with nc.Block() as block:
                @block.tensor
                def _(pe):
                    pe_ffn_credit(pe, s)
                    stats_pe(pe, s, b, UNITS, True)
                    for u in range(UNITS):
                        norm_pe(pe, s, b, UNITS + u, u % 2)

                @block.gpsimd
                def _(pool):
                    pool_ffn_credit(pool, s)
                    stats_pool(pool, s, b, UNITS)

                @block.vector
                def _(dve):
                    dve_ffn_credit(dve, s)
                    stats_dve(dve, s, b, UNITS, True)
                    rstd_dve(dve, s, b, UNITS, NEWTON_OPS + 1)
                    for u in range(UNITS):
                        norm_dve_diag(dve, s, b, UNITS + u, NEWTON_OPS + 1, u, u % 2)
                        norm_dve(dve, s, b, UNITS + u, u, b.X)

        layer_norm("ln0")
        with nc.Block() as block:
            @block.vector
            def _(dve):
                dve.memset(vbuf[:, :], 0.0)
        s0 = AttentionSems(ctx, nc, "first")
        pe0, act0, dve0, pool0 = attention_programs(g0, s0, b)
        with nc.Block() as block:
            @block.tensor
            def _(pe):
                pe_credit(pe, g0, s0)
                pe0(pe, FIRST_N)

            @block.scalar
            def _(act):
                act_credit(act, g0, s0)
                act0(act, FIRST_N)

            @block.vector
            def _(dve):
                dve_credit(dve, g0, s0)
                dve0(dve, FIRST_N)

            @block.gpsimd
            def _(pool):
                pool_credit(pool, g0, s0)
                pool0(pool, FIRST_N)
        layer_norm("ln1")

        s1 = AttentionSems(ctx, nc, "deep")
        f1 = FfnSems(ctx, nc, "ffn")
        pe1, act1, dve1, pool1 = attention_programs(g1, s1, b)
        w_loaded, w_hi, w_ready = sem("w_loaded"), sem("w_hi"), sem("w_ready")
        xs_zero = sem("xs_zero")
        with nc.Block() as block:
            @block.vector
            def _(dve):
                dve.memset(b.kh[:, :, :, 0:WINDOW], 0.0)
                dve.memset(b.kl[:, :, :, 0:WINDOW], 0.0)
                dve.memset(b.xh[:, :, 0:WINDOW + 1], 0.0)
                dve.memset(b.xl[:, :, 0:WINDOW + 1], 0.0)
        with nc.Block() as block:
            @block.sync
            def _(sp):
                with sp.Fori(0, DEPTH) as l:
                    sp.wait_ge(w_ready, l * 3 + 1)
                    one = bass.ds(l, 1)
                    sp.dma_start(watt_f[:, 0:3 * INNER], wqkv[one, :, :].rearrange("a p d -> p (a d)")).then_inc(w_loaded, 16)
                    sp.dma_start(watt_f[:, 3 * INNER:].rearrange("p (c d) -> p c d", c=INNER // P),
                                 wo[one, :, :].rearrange("a (c p) d -> p (a c) d", p=P)).then_inc(w_loaded, 16)
                    sp.dma_start(wffn_f[:, 0:2 * DIM_INNER], w1[one, :, :].rearrange("a p d -> p (a d)")).then_inc(w_loaded, 16)
                    sp.dma_start(wffn_f[:, 2 * DIM_INNER:].rearrange("p (c d) -> p c d", c=NF),
                                 w2[one, :, :].rearrange("a (c p) d -> p (a c) d", p=P)).then_inc(w_loaded, 16)
                    sp.dma_start(qks_sb[:, :, :], qks[one, :, :, :].rearrange("a p k d -> p (a k) d")).then_inc(w_loaded, 16)

            @block.tensor
            def _(pe):
                pe_credit(pe, g1, s1)
                pe_ffn_credit(pe, f1)
                with pe.Fori(0, DEPTH) as l:
                    pe.wait_ge(w_ready, l * 3 + 4)
                    pe1(pe, pe.snap(l * SEQS + FIRST_N))
                    base = pe.snap(l * UNITS + UNITS)
                    stats_pe(pe, f1, b, base, False)
                    ffn_units(pe, base,
                              lambda bu, b3, u, par: norm_pe(pe, f1, b, bu, par),
                              lambda bu, b3, u, par: up_pe(pe, f1, b, bu, b3, par),
                              lambda bu, b3, u, par: down_pe(pe, f1, b, bu, b3, par))

            @block.scalar
            def _(act):
                act_credit(act, g1, s1)
                act_ffn_credit(act, f1)
                with act.Fori(0, DEPTH) as l:
                    act.wait_ge(w_loaded, l * 80 + 80)
                    act.wait_ge(f1.residual, l * UNITS + UNITS)
                    act.activation(watt[0][:, :], watt_f[:, :], ACT.Copy).then_inc(w_hi, 1)
                    act.activation(wffn[0][:, :], wffn_f[:, :], ACT.Copy).then_inc(w_hi, 1)
                    act1(act, act.snap(l * SEQS + FIRST_N))
                    act.wait_ge(s1.residual, l * SEQS + SEQS + FIRST_N)
                    act.activation(b.xs[64:P, :, :].rearrange("p s (q t) -> p (s q) t", t=N_TOK)[:, :, 0:1],
                                   b.ident[64:P, 0:4].unsqueeze(2), ACT.Copy, scale=0.0).then_inc(xs_zero, 1)
                    stats_act(act, f1, b, l)
                    base = act.snap(l * UNITS + UNITS)
                    ffn_units(act, base,
                              lambda bu, b3, u, par: affine_act(act, f1, b, bu, u, par),
                              lambda bu, b3, u, par: gelu_act(act, f1, b, b3, par),
                              lambda bu, b3, u, par: None)

            @block.vector
            def _(dve):
                dve_credit(dve, g1, s1)
                dve.sem_inc(w_ready, 1)
                dve_ffn_credit(dve, f1)
                with dve.Fori(0, DEPTH) as l:
                    dve.wait_ge(w_hi, l * 2 + 1)
                    dve.tensor_tensor(watt[1][:, :], watt_f[:, :], watt[0][:, :], ALU.subtract).then_inc(w_ready, 1)
                    dve.wait_ge(w_hi, l * 2 + 2)
                    dve.tensor_tensor(wffn[1][:, :], wffn_f[:, :], wffn[0][:, :], ALU.subtract).then_inc(w_ready, 1)
                    dve.tensor_tensor(b.table[:, :, :, :], rope_sb[:, :, :, :],
                                      qks_sb[:, :, :].unsqueeze(1).broadcast_to([P, 2, 4, DIM_HEAD]), ALU.mult)
                    dve.tensor_copy(b.vec[:, :], vecs_sb[:, bass.ds(l, 1), :].rearrange("p a v -> p (a v)")).then_inc(w_ready, 1)
                    dve.wait_ge(w_ready, l * 3 + 4)
                    dve1(dve, dve.snap(l * SEQS + FIRST_N))
                    base = dve.snap(l * UNITS + UNITS)
                    base_newton = dve.snap(l * (NEWTON_OPS + 1) + NEWTON_OPS + 1)
                    stats_dve(dve, f1, b, base, False)
                    rstd_dve(dve, f1, b, base, base_newton)

                    def norm(bu, b3, u, par):
                        norm_dve_diag(dve, f1, b, bu, base_newton, u, par)
                        norm_dve(dve, f1, b, bu, u, b.xc)
                        affine_dve_hi(dve, f1, b, bu, b3, par)

                    ffn_units(dve, base, norm,
                              lambda bu, b3, u, par: gate_dve(dve, f1, b, bu, b3, par),
                              lambda bu, b3, u, par: down_dve(dve, f1, b, bu, u, par))

            @block.gpsimd
            def _(pool):
                pool_credit(pool, g1, s1)
                pool_ffn_credit(pool, f1)
                with pool.Fori(0, DEPTH) as l:
                    pool1(pool, pool.snap(l * SEQS + FIRST_N))
                    base = pool.snap(l * UNITS + UNITS)
                    stats_pool(pool, f1, b, base)
                    ffn_units(pool, base,
                              lambda bu, b3, u, par: affine_pool_lo(pool, f1, b, bu, par),
                              lambda bu, b3, u, par: gate_pool_lo(pool, f1, b, b3, par),
                              lambda bu, b3, u, par: None)

        summed, stored = sem("summed"), sem("stored")
        with nc.Block() as block:
            @block.vector
            def _(dve):
                for u in range(UNITS):
                    dve.tensor_tensor(unit(b.X1, u), unit(b.X1, u), unit(b.X, u), ALU.add).then_inc(summed, 1)

            @block.sync
            def _(sp):
                for u in range(UNITS):
                    sp.wait_ge(summed, u + 1)
                    sp.dma_start(unit(out_t, u), unit(b.X1, u)).then_inc(stored, 16)
                sp.wait_ge(stored, 16 * UNITS)


def constants():
    f = np.float32
    big = -1e30
    q, k = np.arange(BLOCK_Q)[:, None], np.arange(BLOCK_K)[None, :]
    masks = np.zeros((P, 5, BLOCK_K), f)
    for t in range(2):
        for half in range(2):
            blk = 2 * t + half
            rows = slice(64 * half, 64 * half + 64)
            pos = 64 * blk + k - 16
            lo = 32 * (q // 32)
            ok = (k >= lo) & (k < lo + 64) & (pos >= 0) & (pos < N_TOK)
            masks[rows, t] = np.where(ok, 0.0, big)
            i, j = 64 * blk + q, 64 * blk + k - 32
            same = (j // 32 == i // 32) | (j // 32 == i // 32 - 1)
            ok = same & (j >= 0) & (i >= j) & (i <= j + 32)
            masks[rows, 2 + t] = np.where(ok, 0.0, big)
    half = np.arange(0, DIM_HEAD, 2, dtype=f)
    inv_freq = (f(1.0) / f(10000.0) ** (half / f(DIM_HEAD))).astype(f)
    t = np.arange(N_TOK, dtype=f)
    freqs = t[:, None] * inv_freq[None, :]
    base = ((half + f(0.4 * DIM_HEAD)) / f(1.4 * DIM_HEAD)).astype(f)
    power = (t - N_TOK // 2) / f(WINDOW // 2)
    scale = (base[None, :].astype(np.float64) ** power[:, None]).astype(f)
    cos, sin = np.cos(freqs.astype(np.float64)), np.sin(freqs.astype(np.float64))
    tabs = []
    for sc in (scale.astype(np.float64), 1.0 / scale.astype(np.float64)):
        tabs.append(np.concatenate([cos * sc, cos * sc], 1))
        tabs.append(np.concatenate([-sin * sc, sin * sc], 1))
    rope = np.stack(tabs, 1).astype(f).reshape(2, P, 4, DIM_HEAD).transpose(1, 0, 2, 3)
    rowmask = (np.arange(P)[:, None] % 32 // HEAD_DIM0 == np.arange(4)[None, :]).astype(f)
    return masks, np.eye(P, dtype=f), np.full((P, P), 1.0 / DIM, f), np.ones((P, P), f), rope, rowmask


def kernel(L0_attn_x, L0_attn_w_qkv, L0_attn_b_qkv, L0_attn_w_proj, L0_attn_b_proj, L0_ffn_Wqkv,
           L0_ffn_q_scale, L0_ffn_k_scale, L0_ffn_Wo, L0_ffn_ln_g, L0_ffn_ln_b, L0_ffn_W1, L0_ffn_b1,
           L0_ffn_W2, L0_ffn_b2):
    import concourse.bacc as bacc
    from concourse.bass_utils import run_bass_kernel_spmd

    def arr(a):
        return np.ascontiguousarray(np.asarray(a))

    masks, ident, inv_dim, ones, rope, rowmask = constants()
    x = arr(L0_attn_x)
    bq = arr(L0_attn_b_qkv)
    qs, ks = arr(L0_ffn_q_scale), arr(L0_ffn_k_scale)
    swap = np.roll(np.arange(DIM_HEAD), DIM_HEAD // 2)
    qks = np.stack([qs, qs[:, swap], ks, ks[:, swap]], 1)[:, None]
    b1 = arr(L0_ffn_b1)
    b1p = np.zeros((DEPTH, 2, NF * P), b1.dtype)
    b1p[:, :, :DIM_INNER] = b1.reshape(DEPTH, 2, DIM_INNER)
    w2 = arr(L0_ffn_W2)
    w2p = np.zeros((DEPTH, NF * P, DIM), w2.dtype)
    w2p[:, :DIM_INNER] = w2
    vecs = np.concatenate([arr(L0_ffn_ln_g)[:, None], arr(L0_ffn_ln_b)[:, None],
                           b1p.reshape(DEPTH, 2 * NF, P), arr(L0_ffn_b2)[:, None]], 1)
    arrays = {
        "x_t": x.reshape(TOKENS, DIM).T, "w0": arr(L0_attn_w_qkv).T, "wo0": arr(L0_attn_w_proj).T,
        "vec0": np.stack([bq[:DIM], bq[DIM:2 * DIM], arr(L0_attn_b_proj)], 1),
        "vbias": np.broadcast_to(bq[2 * DIM:], (BLOCK_K, DIM)), "masks": masks, "ident": ident,
        "inv_dim": inv_dim, "ones": ones, "rope": rope, "rowmask": rowmask, "wqkv": arr(L0_ffn_Wqkv),
        "qks": np.broadcast_to(qks, (DEPTH, P, 4, DIM_HEAD)), "wo": arr(L0_ffn_Wo), "w1": arr(L0_ffn_W1),
        "w2": w2p, "vecs": vecs.transpose(2, 0, 1),
    }
    arrays = {k: np.ascontiguousarray(v) for k, v in arrays.items()}
    nc = bacc.Bacc("TRN2", target_bir_lowering=False, num_devices=1)
    args = {k: nc.dram_tensor(f"in_{k}", v.shape, mybir.dt.from_np(v.dtype), kind="ExternalInput").ap()
            for k, v in arrays.items()}
    out = nc.dram_tensor("out_t", (DIM, TOKENS), F32, kind="ExternalOutput").ap()
    build(nc, **args, out_t=out)
    r = run_bass_kernel_spmd(nc, [{f"in_{k}": v for k, v in arrays.items()}], core_ids=[0])
    return r.results[0]["out_t"].T.reshape(x.shape)
```

```python
from contextlib import ExitStack

import numpy as np

import concourse.bass as bass
from concourse import mybir

ALU = mybir.AluOpType
ACT = mybir.ActivationFunctionType
F32 = mybir.dt.float32
BF16 = mybir.dt.bfloat16
I32 = mybir.dt.int32
AX_X = mybir.AxisListType.X

P = 128
SEQS, N_TOK, DIM = 16, 256, 128
TOKENS = SEQS * N_TOK
DEPTH = 6
HEADS, DIM_HEAD = 16, 64
INNER = HEADS * DIM_HEAD
DIM_INNER = int(DIM * 4 * 2 / 3)
HEAD_DIM0 = DIM // HEADS
SCALE0 = HEAD_DIM0 ** -0.5
QK_SCALE = 8.0
WINDOW = 32
BLOCK_Q = 64
BLOCK_K = BLOCK_Q + WINDOW
BLOCKS = N_TOK // BLOCK_Q
PADDED = N_TOK + WINDOW
QUADS = 8
UNIT = 512
UNITS = TOKENS // UNIT
LN_EPS = 1e-5
RSQRT_MAGIC = 1597463007.0
NEWTON_OPS = 11
FIRST_N = 2
F_CHUNKS = [(c * P, min(P, DIM_INNER - c * P)) for c in range(-(-DIM_INNER // P))]
NF = len(F_CHUNKS)

DEEP_STEPS = [
    ([("PJ", 0)], [("PJ", 1)], []),
    ([("PJ", 2)], [("PJ", 3)], []),
    ([("PJ", 4)], [], []),
    ([("PJ", 5), ("V", 0)], [("V", 1)], [("V", 2)]),
    ([("PJ", 6)], [("TK", 0)], [("V", 3)]),
    ([], [("TQ", 0), ("PJ", 7), ("TK", 1)], []),
    ([("TQ", 1)], [("TK", 2)], [("V", 4), ("V", 5)]),
    ([], [("V", 6), ("TQ", 2), ("TQ", 3)], [("V", 7), ("TK", 3)]),
]
FIRST_STEPS = [
    ([("Q", 0)], [], []), ([("K", 0)], [], []), ([], [], [("V0", 0)]), ([], [], [("V0", 1)]),
    ([], [], [("V0", 2)]), ([], [], [("V0", 3)]), ([], [], []), ([], [], []),
]
STEPS = QUADS
EXP_LAG, PT_LAG, PV_LAG = 1, 2, 3
PROJECT_STEP = 3
INPUT_STEP = 4
DRAIN = PROJECT_STEP + 1


class Geometry:

    def __init__(self, first):
        self.first = first
        self.steps = FIRST_STEPS if first else DEEP_STEPS
        order = [item for step in self.steps for place in step for item in place]
        assert len(order) % 3 == 0
        self.order = order
        self.index = {item: j for j, item in enumerate(order)}
        self.act_index = {item: j for j, item in enumerate(i for i in order if i[0] != "V0")}
        self.dve_index = {item: j for j, item in enumerate(i for i in order if i[0] not in ("V", "Q", "K"))}
        self.acts, self.dves = len(self.act_index), len(self.dve_index)
        self.items = len(order)
        self.quads_per_out = 4 if first else 2
        self.outs = QUADS // self.quads_per_out
        self.chunks = 1 if first else INNER // P
        self.lead = WINDOW // 2 if first else WINDOW


class Buffers:
    pass


def counts(e, n, pers):
    if isinstance(n, int):
        c = {per: n * per for per in pers}
    else:
        c = {per: (e.snap(n * per) if per > 1 else n) for per in pers}
    return c, {per: v - per for per, v in c.items()}, {per: v + per for per, v in c.items()}


def bf16_parts_matmul(e, out, stat, moving, start, stop, skip=False):
    (sh, sl), (mh, ml) = stat, moving
    e.matmul(out, sh, mh, start=start, stop=False, skip_group_check=skip)
    e.matmul(out, sh, ml, start=False, stop=False, skip_group_check=skip)
    return e.matmul(out, sl, mh, start=False, stop=stop, skip_group_check=skip)


def rsqrt_op(e, i, x, y, a, src, floor, scale):
    if i == 0:
        return e.tensor_scalar(x, src, floor, scale, ALU.max, ALU.mult)
    if i == 1:
        return e.tensor_scalar(y.bitcast(I32), x.bitcast(I32), -0.5, RSQRT_MAGIC, ALU.mult, ALU.add)
    if i % 3 == 2:
        return e.tensor_tensor(a, y, y, ALU.mult)
    if i % 3 == 0:
        return e.scalar_tensor_tensor(a, a, -0.5, x, ALU.mult, ALU.mult)
    return e.scalar_tensor_tensor(y, a, 1.5, y, ALU.add, ALU.mult)


def quad_heads(g, m):
    t, quad = divmod(m, 4)
    if g.first:
        return t, 32 * quad, 32, [(r, 4 * quad + r) for r in range(4)]
    half, odd = divmod(quad, 2)
    return t, 64 * odd, 64, [(4 * half + j, 8 * half + 2 * j + odd) for j in range(4)]



class AttentionSems:

    def __init__(self, ctx, nc, tag):
        def sem(name):
            return ctx.enter_context(nc.semaphore(f"{tag}_{name}"))

        self.x_hi = sem("x_hi")
        self.x_lo = sem("x_lo")
        self.work_full = sem("work_full")
        self.work_read = sem("work_read")
        self.work_free = sem("work_free")
        self.rotated = sem("rotated")
        self.newton = sem("newton")
        self.k_scaled = sem("k_scaled")
        self.scores = sem("scores")
        self.row_max = sem("row_max")
        self.neg_max = sem("neg_max")
        self.exps = sem("exps")
        self.recip = sem("recip")
        self.probs = sem("probs")
        self.pt_full = sem("pt_full")
        self.pt_copied = sem("pt_copied")
        self.pv_full = sem("pv_full")
        self.out_hi = sem("out_hi")
        self.out_lo = sem("out_lo")
        self.proj_full = sem("proj_full")
        self.residual = sem("residual")


def pe_credit(e, g, s):
    e.sem_inc(s.work_full, FIRST_N * g.items)
    e.sem_inc(s.scores, FIRST_N * 8)
    e.sem_inc(s.pt_full, FIRST_N * 8)
    e.sem_inc(s.pv_full, FIRST_N * 8)
    e.sem_inc(s.proj_full, FIRST_N)


def act_credit(e, g, s):
    e.sem_inc(s.x_hi, FIRST_N * 2)
    e.sem_inc(s.work_read, FIRST_N * g.acts)
    e.sem_inc(s.exps, FIRST_N * 8)
    e.sem_inc(s.pt_copied, FIRST_N * 8)
    e.sem_inc(s.out_hi, FIRST_N * g.outs)


def dve_credit(e, g, s):
    e.sem_inc(s.x_lo, FIRST_N * 2)
    e.sem_inc(s.work_free, FIRST_N * g.dves)
    e.sem_inc(s.newton, FIRST_N * 2 * NEWTON_OPS)
    e.sem_inc(s.row_max, FIRST_N * 8)
    e.sem_inc(s.neg_max, FIRST_N * 8)
    e.sem_inc(s.recip, FIRST_N * 8)
    e.sem_inc(s.out_lo, FIRST_N * g.outs)
    e.sem_inc(s.residual, FIRST_N)


def pool_credit(e, g, s):
    e.sem_inc(s.rotated, FIRST_N * 8)
    e.sem_inc(s.k_scaled, FIRST_N * 4)
    e.sem_inc(s.probs, FIRST_N * 8)


def pe_item(e, g, s, b, item, c, nxt):
    kind, u = item
    j = g.index[item]
    bank = b.work[j % 3]
    before = g.order[j - 3]
    if before in g.dve_index:
        e.wait_ge(s.work_free, c[g.dves] + g.dve_index[before] + 1 - (g.dves if j < 3 else 0))
    else:
        e.wait_ge(s.work_read, c[g.acts] + g.act_index[before] + 1 - (g.acts if j < 3 else 0))
    if kind == "PJ":
        isq, t, half = u // 4, (u % 4) // 2, u % 2
        col = (0 if isq else INNER) + 512 * half
        tok = slice(g.lead + P * t, g.lead + P * (t + 1))
        for k, (xp, wp) in enumerate([(b.xh, b.wh), (b.xh, b.wl), (b.xl, b.wh)]):
            mm = e.matmul(bank[:, :], xp[:, nxt, tok], wp[:, col:col + 512], start=(k == 0), stop=(k == 2))
    elif kind == "V":
        blk, half = divmod(u, 2)
        col = 2 * INNER + 512 * half
        tok = slice(BLOCK_Q * blk, BLOCK_Q * blk + BLOCK_K)
        for k, (xp, wp) in enumerate([(b.xh, b.wh), (b.xh, b.wl), (b.xl, b.wh)]):
            mm = e.matmul(bank[0:BLOCK_K, :], xp[:, nxt, tok], wp[:, col:col + 512], start=(k == 0), stop=(k == 2))
    elif kind in ("TQ", "TK"):
        if kind == "TQ":
            e.wait_ge(s.rotated, c[8] + 4 + u + 1)
            src = b.rot[:, 4 + u, :]
        else:
            e.wait_ge(s.k_scaled, c[4] + u + 1)
            src = b.rot[:, u, :]
        for p in range(4):
            mm = e.transpose(bank[:, P * p:P * (p + 1)], src[:, P * p:P * (p + 1)], b.ident[:, :])
    elif kind in ("Q", "K"):
        col = 0 if kind == "Q" else DIM
        tok = slice(g.lead, g.lead + N_TOK)
        mm = e.matmul(bank[:, 0:N_TOK], b.w0[:, col:col + P], b.x0[:, nxt, tok], start=True, stop=True)
    else:
        tok = slice(BLOCK_Q * u, BLOCK_Q * u + BLOCK_K)
        mm = e.matmul(bank[0:BLOCK_K, 0:DIM], b.x0[:, nxt, tok], b.w0[:, 2 * DIM:3 * DIM], start=True, stop=True)
    mm.then_inc(s.work_full, 1)


def pe_scores(e, g, s, b, m, c, par):
    t, row, rows, heads = quad_heads(g, m)
    bank = b.scores[m % 2]
    e.wait_ge(s.exps, c[8] + m - 1)
    if m == 0 and g.first:
        e.wait_ge(s.work_read, c[g.acts] + g.acts)
    elif m == 0:
        e.wait_ge(s.work_free, c[g.dves] + max(g.dve_index[(k, u)] for k in ("TQ", "TK") for u in (0, 1)) + 1)
    elif m == 4 and not g.first:
        e.wait_ge(s.work_free, c[g.dves] + g.dves)
    mask = b.maskb[:, b.mask_of(g, t), :].unsqueeze(1).broadcast_to([P, 4, BLOCK_K])
    e.matmul(bank[:, 0:4 * BLOCK_K].rearrange("p (h k) -> p h k", h=4), b.identb[:, :], mask,
             start=True, stop=False, skip_group_check=True)
    r = slice(row, row + rows)
    for k in range(2):
        blk = 2 * t + k
        for j, (slot, _) in enumerate(heads):
            qs = slice(P * t + BLOCK_Q * k, P * t + BLOCK_Q * (k + 1))
            ks = slice(BLOCK_Q * blk, BLOCK_Q * blk + BLOCK_K)
            out = bank[64 * k:64 * k + 64, BLOCK_K * j:BLOCK_K * (j + 1)]
            stop = k == 1 and j == 3
            if g.first:
                last = e.matmul(out, b.q0[r, par, slot, qs], b.k0[r, par, ks], start=False, stop=stop, skip_group_check=True)
            else:
                last = bf16_parts_matmul(e, out, (b.qh[r, par, slot, qs], b.ql[r, par, slot, qs]),
                                         (b.kh[r, par, slot, ks], b.kl[r, par, slot, ks]), False, stop, skip=True)
    last.then_inc(s.scores, 1)


def pe_transpose_probs(e, g, s, b, m, c):
    e.wait_ge(s.probs, c[8] + m + 1)
    e.wait_ge(s.pt_copied, c[8] + m - 1)
    if m == 2:
        e.wait_ge(s.residual, c[1] + 0)
    for j in range(4):
        mm = e.transpose(b.pt[m % 2][0:BLOCK_K, P * j:P * (j + 1)], b.probs[:, m % 4, j, :], b.ident[:, :])
    mm.then_inc(s.pt_full, 1)


def pe_values(e, g, s, b, m, c, par):
    t, row, rows, heads = quad_heads(g, m)
    e.wait_ge(s.pt_copied, c[8] + m + 1)
    if m == 0:
        if g.first:
            e.wait_ge(s.work_free, c[g.dves] + g.dves)
        else:
            e.wait_ge(s.work_read, c[g.acts] + g.acts)
    if m % g.quads_per_out == 0:
        done = s.out_hi if g.first else s.out_lo
        e.wait_ge(done, c[g.outs] + m // g.quads_per_out)
    for k in range(2):
        blk = 2 * t + k
        for j, (slot, h) in enumerate(heads):
            probs = b.ptf[:, m % 2, P * j + BLOCK_Q * k:P * j + BLOCK_Q * (k + 1)]
            if g.first:
                col = 128 * j + row
                mm = e.matmul(b.out[row:row + 32, BLOCK_Q * k:BLOCK_Q * (k + 1)], b.v[:, par, blk, col:col + 32],
                              probs, start=(j == 0), stop=(j == 3))
            else:
                col = P * (slot % 4) + BLOCK_Q * k
                mm = e.matmul(b.out[row:row + 64, col:col + BLOCK_Q],
                              b.v[:, par, blk, DIM_HEAD * h:DIM_HEAD * (h + 1)], probs, start=True, stop=True)
    mm.then_inc(s.pv_full, 1)


def pe_project(e, g, s, b, c):
    out = b.pt[0][:, 0:N_TOK]
    if g.first:
        e.wait_ge(s.out_hi, c[g.outs] + g.outs)
        mm = e.matmul(out, b.wo0[:, :], b.ot[:, :], start=True, stop=True)
    else:
        e.wait_ge(s.out_lo, c[g.outs] + g.outs)
        for p in range(g.chunks):
            mm = bf16_parts_matmul(e, out, (b.woh[:, p, :], b.wol[:, p, :]), (b.oth[:, p, :], b.otl[:, p, :]),
                                   p == 0, p == g.chunks - 1)
    mm.then_inc(s.proj_full, 1)


def lagging(m, lag, c, cp, par, prev, cur):
    if m >= lag:
        return (m - lag, c, par) if cur else None
    return (m - lag + QUADS, cp, 1 - par) if prev else None


def pe_slot(e, g, s, b, n, par, prev, cur, nxt):
    c, cp, cn = counts(e, n, (g.items, g.acts, g.dves, 8, 4, 2, g.outs, 1))
    for m in range(STEPS if cur else DRAIN):
        places = g.steps[m] if nxt else ([], [], [])
        if nxt and m == 0:
            e.wait_ge(s.x_hi if g.first else s.x_lo, cn[2] + 2)
        for item in places[0]:
            pe_item(e, g, s, b, item, cn, 1 - par)
        if cur:
            pe_scores(e, g, s, b, m, c, par)
        quad = lagging(m, PT_LAG, c, cp, par, prev, cur)
        if quad:
            pe_transpose_probs(e, g, s, b, quad[0], quad[1])
        for item in places[1]:
            pe_item(e, g, s, b, item, cn, 1 - par)
        quad = lagging(m, PV_LAG, c, cp, par, prev, cur)
        if quad:
            pe_values(e, g, s, b, *quad)
        if prev and m == PROJECT_STEP:
            pe_project(e, g, s, b, cp)
        for item in places[2]:
            pe_item(e, g, s, b, item, cn, 1 - par)


def pe_first_items(e, g, s, b, n):
    c, _, _ = counts(e, n, (g.items, g.acts, g.dves, 8, 4, 2))
    e.wait_ge(s.x_hi if g.first else s.x_lo, c[2] + 2)
    for step in g.steps:
        for item in step[0] + step[1] + step[2]:
            pe_item(e, g, s, b, item, c, 0)


def act_input(e, g, s, b, n, seq, par):
    c, _, _ = counts(e, n, (g.items, g.acts, g.dves, 2))
    e.wait_ge(s.work_full, c[g.items] - g.items)
    if g.first:
        e.activation(b.x0[:, par, g.lead:g.lead + N_TOK], b.X[:, bass.ds(seq * N_TOK, N_TOK)], ACT.Copy).then_inc(s.x_hi, 2)
    else:
        e.activation(b.xh[0:64, par, g.lead:PADDED], b.X[0:64, bass.ds(seq * N_TOK, N_TOK)], ACT.Copy).then_inc(s.x_hi, 1)
        e.activation(b.xh[64:P, par, g.lead + 1:PADDED], b.X[64:P, bass.ds(seq * N_TOK, N_TOK - 1)], ACT.Copy).then_inc(s.x_hi, 1)


def dve_input(e, g, s, b, n, seq, par):
    if g.first:
        return
    c, _, _ = counts(e, n, (2,))
    a = g.lead
    for k, (r, d) in enumerate([(slice(0, 64), 0), (slice(64, P), 1)]):
        e.wait_ge(s.x_hi, c[2] + k + 1)
        e.tensor_tensor(b.xl[r, par, a + d:a + N_TOK], b.X[r, bass.ds(seq * N_TOK, N_TOK - d)],
                        b.xh[r, par, a + d:a + N_TOK], ALU.subtract).then_inc(s.x_lo, 1)


def act_item(e, g, s, b, item, c, nxt):
    kind, u = item
    j = g.index[item]
    bank = b.work[j % 3]
    if kind == "V0":
        return
    e.wait_ge(s.work_full, c[g.items] + j + 1)
    if kind == "PJ":
        if u >= 2:
            e.wait_ge(s.work_free, c[g.dves] + g.dve_index[("PJ", u - 2)] + 1)
        e.activation(b.sq[:, u % 2, :], bank[:, :], ACT.Square).then_inc(s.work_read, 1)
    elif kind == "V":
        blk, half = divmod(u, 2)
        e.activation(b.v[:, nxt, blk, 512 * half:512 * (half + 1)], bank[0:BLOCK_K, :], ACT.Copy).then_inc(s.work_read, 1)
    elif kind in ("TQ", "TK"):
        t, half = divmod(u, 2)
        dst, off = (b.qh, 0) if kind == "TQ" else (b.kh, g.lead)
        e.activation(dst[:, nxt, 4 * half:4 * half + 4, off + P * t:off + P * (t + 1)],
                     bank[:, :].rearrange("p (h t) -> p h t", h=4), ACT.Copy).then_inc(s.work_read, 1)
    elif kind == "Q":
        for r in range(4):
            op = e.activation(b.q0[:, nxt, r, :], bank[:, 0:N_TOK], ACT.Identity, bias=b.qbias[:, r:r + 1],
                              scale=b.rowmask[:, r:r + 1])
        op.then_inc(s.work_read, 1)
    else:
        e.activation(b.k0[:, nxt, g.lead:g.lead + N_TOK], bank[:, 0:N_TOK], ACT.Identity, bias=b.qkb[:, 1:2]).then_inc(s.work_read, 1)


def first_values(v, par, blk):
    flat = v[:, par, blk, 0:4 * (DIM + HEAD_DIM0)].rearrange("p (r x) -> p r x", r=4)
    return flat[:, :, 0:128].rearrange("p r (g y) -> p r g y", g=4)[:, :, :, 0:HEAD_DIM0]


def act_exp(e, g, s, b, m, c, par):
    t, row, rows, heads = quad_heads(g, m)
    if m == 0 and not g.first:
        e.wait_ge(s.newton, c[2 * NEWTON_OPS] + 2 * NEWTON_OPS)
    e.wait_ge(s.neg_max, c[8] + m + 1)
    e.wait_ge(s.pt_full, c[8] + m - 3)
    for j, (_, h) in enumerate(heads):
        scale = SCALE0 if g.first else b.rq[:, par, t * HEADS + h:t * HEADS + h + 1]
        op = e.activation(b.probs[:, m % 4, j, :], b.scores[m % 2][:, BLOCK_K * j:BLOCK_K * (j + 1)], ACT.Exp,
                          bias=b.nmax[:, m % 2, j:j + 1], scale=scale, accum_out=b.den[:, m % 4, j:j + 1])
    op.then_inc(s.exps, 1)


def act_copy_pt(e, g, s, b, m, c):
    e.wait_ge(s.pt_full, c[8] + m + 1)
    e.wait_ge(s.pv_full, c[8] + m - 1)
    e.activation(b.ptf[:, m % 2, :], b.pt[m % 2][0:BLOCK_K, :], ACT.Copy).then_inc(s.pt_copied, 1)


def out_views(g, b, i, part):
    t, half = divmod(i, 2)
    return (part[:, 4 * half:4 * half + 4, P * t:P * (t + 1)],
            b.out[:, :].rearrange("p (h t) -> p h t", h=4))


def act_out_hi(e, g, s, b, i, c):
    e.wait_ge(s.pv_full, c[8] + g.quads_per_out * (i + 1))
    if i == 0:
        e.wait_ge(s.proj_full, c[1] + 0)
    if g.first:
        e.activation(b.ot[:, P * i:P * (i + 1)], b.out[:, 0:P], ACT.Copy).then_inc(s.out_hi, 1)
    else:
        dst, src = out_views(g, b, i, b.oth)
        e.activation(dst, src, ACT.Copy).then_inc(s.out_hi, 1)


def out_number(g, quad):
    return quad // g.quads_per_out if (quad + 1) % g.quads_per_out == 0 else None


def act_slot(e, g, s, b, n, seq, par, prev, cur, nxt, with_input):
    c, cp, cn = counts(e, n, (g.items, g.acts, g.dves, 8, 4, 2, g.outs, 1, 2 * NEWTON_OPS))
    for m in range(STEPS if cur else DRAIN):
        places = g.steps[m] if nxt else ([], [], [])
        quad = lagging(m, EXP_LAG, c, cp, par, prev, cur)
        if quad:
            act_exp(e, g, s, b, *quad)
        for item in places[0]:
            act_item(e, g, s, b, item, cn, 1 - par)
        for item in places[1]:
            act_item(e, g, s, b, item, cn, 1 - par)
        quad = lagging(m, PT_LAG, c, cp, par, prev, cur)
        if quad:
            act_copy_pt(e, g, s, b, quad[0], quad[1])
        quad = lagging(m, PV_LAG, c, cp, par, prev, cur)
        if quad and out_number(g, quad[0]) is not None:
            act_out_hi(e, g, s, b, out_number(g, quad[0]), quad[1])
        for item in places[2]:
            act_item(e, g, s, b, item, cn, 1 - par)
        if with_input and m == INPUT_STEP:
            act_input(e, g, s, b, n + 2, seq + 2, par)


def act_first_items(e, g, s, b, n, seq):
    act_input(e, g, s, b, n, seq, 0)
    act_input(e, g, s, b, n + 1, seq + 1, 1)
    c, _, _ = counts(e, n, (g.items, g.acts, g.dves, 4, 1))
    for step in g.steps:
        for item in step[0] + step[1] + step[2]:
            act_item(e, g, s, b, item, c, 0)


def dve_item(e, g, s, b, item, c, nxt):
    kind, u = item
    j = g.index[item]
    bank = b.work[j % 3]
    if item not in g.dve_index:
        return
    if kind == "V0":
        e.wait_ge(s.work_full, c[g.items] + j + 1)
    else:
        e.wait_ge(s.work_read, c[g.acts] + g.act_index[item] + 1)
    if kind == "PJ":
        isq, t, half = u // 4, (u % 4) // 2, u % 2
        col = (0 if isq else 2 * HEADS) + HEADS * t + 8 * half
        e.tensor_reduce(b.ss[:, nxt, col:col + 8], b.sq[:, u % 2, :].rearrange("p (h d) -> p h d", h=8), AX_X, ALU.add)
        pj = bank[:, :].rearrange("p (h s d) -> p h s d", h=8, s=2)
        first = 0 if isq else 2
        cos = b.table[:, t, first, :].rearrange("p (s d) -> p s d", s=2).unsqueeze(1).broadcast_to([P, 8, 2, 32])
        sin = b.table[:, t, first + 1, :].rearrange("p (s d) -> p s d", s=2).unsqueeze(1).broadcast_to([P, 8, 2, 32])
        e.wait_ge(s.rotated, c[8] + u - 1)
        e.tensor_tensor(b.m1[:, u % 2, :].rearrange("p (h s d) -> p h s d", h=8, s=2), pj, cos, ALU.mult)
        e.tensor_tensor(b.m2[:, u % 2, :].rearrange("p (h s d) -> p h s d", h=8, s=2), pj[:, :, ::-1, :], sin,
                        ALU.mult).then_inc(s.work_free, 1)
    elif kind in ("TQ", "TK"):
        t, half = divmod(u, 2)
        hi, lo, off = (b.qh, b.ql, 0) if kind == "TQ" else (b.kh, b.kl, g.lead)
        where = (slice(None), nxt, slice(4 * half, 4 * half + 4), slice(off + P * t, off + P * (t + 1)))
        e.tensor_tensor(lo[where], bank[:, :].rearrange("p (h t) -> p h t", h=4), hi[where],
                        ALU.subtract).then_inc(s.work_free, 1)
    else:
        e.tensor_tensor(first_values(b.v, nxt, u), bank[0:BLOCK_K, 0:DIM].rearrange("p (g r d) -> p r g d", g=4, r=4),
                        b.vbias[:, :].rearrange("p (g r d) -> p r g d", g=4, r=4), ALU.add).then_inc(s.work_free, 1)


def dve_newton(e, g, s, b, i, c, nxt):
    isq, op = divmod(i, NEWTON_OPS)
    cols = slice(0, 2 * HEADS) if isq else slice(2 * HEADS, 4 * HEADS)
    if op == 0:
        last = g.dve_index[("PJ", 7 if isq else 3)]
        e.wait_ge(s.work_free, c[g.dves] + last + 1)
    e.wait_ge(s.newton, c[2 * NEWTON_OPS] + i)
    x, a = b.nx[:, cols], b.na[:, cols]
    y = b.rq[:, nxt, :] if isq else b.rk[:, :]
    scale = 1.0 / (QK_SCALE * QK_SCALE) if isq else 1.0
    rsqrt_op(e, op, x, y, a, b.ss[:, nxt, cols], 1e-24, scale).then_inc(s.newton, 1)


def dve_max(e, g, s, b, m, c, par):
    t, row, rows, heads = quad_heads(g, m)
    e.wait_ge(s.scores, c[8] + m + 1)
    e.tensor_reduce(b.rmax[:, m % 2, :], b.scores[m % 2][:, 0:4 * BLOCK_K].rearrange("p (h k) -> p h k", h=4),
                    AX_X, ALU.max).then_inc(s.row_max, 1)
    e.wait_ge(s.row_max, c[8] + m + 1)
    if g.first:
        e.tensor_scalar(b.nmax[:, m % 2, :], b.rmax[:, m % 2, :], -SCALE0, None, ALU.mult).then_inc(s.neg_max, 1)
    else:
        h0 = t * HEADS + heads[0][1]
        e.scalar_tensor_tensor(b.nmax[:, m % 2, :], b.rmax[:, m % 2, :], -1.0, b.rq[:, par, h0:h0 + 7:2],
                               ALU.mult, ALU.mult).then_inc(s.neg_max, 1)


def dve_recip(e, g, s, b, m, c):
    e.wait_ge(s.exps, c[8] + m + 1)
    e.reciprocal(b.rden[:, m % 4, :], b.den[:, m % 4, :]).then_inc(s.recip, 1)


def dve_out_lo(e, g, s, b, i, c):
    e.wait_ge(s.out_hi, c[g.outs] + i + 1)
    dst, src = out_views(g, b, i, b.otl)
    hi, _ = out_views(g, b, i, b.oth)
    e.tensor_tensor(dst, src, hi, ALU.subtract).then_inc(s.out_lo, 1)


def dve_residual(e, g, s, b, c, seq):
    e.wait_ge(s.proj_full, c[1] + 1)
    if g.first:
        x = b.X1[:, bass.ds(seq * N_TOK, N_TOK)]
        e.scalar_tensor_tensor(x, b.pt[0][:, 0:N_TOK], b.qkb[:, 2:3], x, ALU.add, ALU.add).then_inc(s.residual, 1)
    else:
        x = b.X[:, bass.ds(seq * N_TOK, N_TOK)]
        e.tensor_tensor(x, b.pt[0][:, 0:N_TOK], x, ALU.add).then_inc(s.residual, 1)


NEWTON_AT = {2: range(0, 5), 3: range(5, 11), 6: range(11, 17), 7: range(17, 22)}


def dve_slot(e, g, s, b, n, seq, par, prev, cur, nxt, with_input):
    c, cp, cn = counts(e, n, (g.items, g.acts, g.dves, 8, 4, 2, g.outs, 1, 2 * NEWTON_OPS))
    for m in range(STEPS if cur else DRAIN):
        places = g.steps[m] if nxt else ([], [], [])
        newton = list(NEWTON_AT.get(m, ())) if nxt and not g.first else []

        def step_newton():
            if newton:
                dve_newton(e, g, s, b, newton.pop(0), cn, 1 - par)

        if cur:
            dve_max(e, g, s, b, m, c, par)
        step_newton()
        quad = lagging(m, EXP_LAG, c, cp, par, prev, cur)
        if quad:
            dve_recip(e, g, s, b, quad[0], quad[1])
        step_newton()
        for item in places[0]:
            dve_item(e, g, s, b, item, cn, 1 - par)
        step_newton()
        for item in places[1]:
            dve_item(e, g, s, b, item, cn, 1 - par)
        step_newton()
        quad = lagging(m, PV_LAG, c, cp, par, prev, cur)
        if quad and not g.first and out_number(g, quad[0]) is not None:
            dve_out_lo(e, g, s, b, out_number(g, quad[0]), quad[1])
        step_newton()
        for item in places[2]:
            dve_item(e, g, s, b, item, cn, 1 - par)
        if prev and m == PROJECT_STEP:
            dve_residual(e, g, s, b, cp, seq - 1)
        if with_input and m == INPUT_STEP:
            dve_input(e, g, s, b, n + 2, seq + 2, par)
        while newton:
            step_newton()


def dve_first_items(e, g, s, b, n, seq):
    dve_input(e, g, s, b, n, seq, 0)
    dve_input(e, g, s, b, n + 1, seq + 1, 1)
    c, _, _ = counts(e, n, (g.items, g.acts, g.dves, 8, 4, 2 * NEWTON_OPS))
    for m, step in enumerate(g.steps):
        for item in step[0] + step[1] + step[2]:
            dve_item(e, g, s, b, item, c, 0)
        if not g.first:
            for i in NEWTON_AT.get(m, ()):
                dve_newton(e, g, s, b, i, c, 0)


def pool_rotate(e, g, s, b, u, c):
    e.wait_ge(s.work_free, c[g.dves] + g.dve_index[("PJ", u)] + 1)
    e.wait_ge(s.work_full, c[g.items] + g.index[("TQ", u - 4) if u >= 4 else ("TK", u)] + 1 - g.items)
    e.tensor_tensor(b.rot[:, u, :], b.m1[:, u % 2, :], b.m2[:, u % 2, :], ALU.add).then_inc(s.rotated, 1)


def pool_scale_k(e, g, s, b, u, c):
    if u == 0:
        e.wait_ge(s.newton, c[2 * NEWTON_OPS] + NEWTON_OPS)
        e.wait_ge(s.rotated, c[8] + 4)
    t, half = divmod(u, 2)
    rk = b.rk[:, t * HEADS + 8 * half:t * HEADS + 8 * half + 8].unsqueeze(2).broadcast_to([P, 8, DIM_HEAD])
    v = b.rot[:, u, :].rearrange("p (h d) -> p h d", h=8)
    e.tensor_tensor(v, v, rk, ALU.mult).then_inc(s.k_scaled, 1)


def pool_normalise(e, g, s, b, m, c):
    e.wait_ge(s.recip, c[8] + m + 1)
    p = b.probs[:, m % 4, :, :]
    e.tensor_tensor(p, p, b.rden[:, m % 4, :].unsqueeze(2).broadcast_to([P, 4, BLOCK_K]), ALU.mult).then_inc(s.probs, 1)


SCALE_K_AT = {3: (0, 1), 4: (2,), 5: (3,)}


def pool_items(e, g, s, b, m, c):
    if g.first:
        return
    for u in SCALE_K_AT.get(m, ()):
        pool_scale_k(e, g, s, b, u, c)
    for kind, u in g.steps[m][0] + g.steps[m][1] + g.steps[m][2]:
        if kind == "PJ":
            pool_rotate(e, g, s, b, u, c)


def pool_slot(e, g, s, b, n, prev, cur, nxt):
    c, cp, cn = counts(e, n, (g.items, g.acts, g.dves, 8, 4, 2 * NEWTON_OPS))
    for m in range(STEPS if cur else DRAIN):
        quad = lagging(m, EXP_LAG, c, cp, 0, prev, cur)
        if quad:
            pool_normalise(e, g, s, b, quad[0], quad[1])
        if nxt:
            pool_items(e, g, s, b, m, cn)


def pool_first_items(e, g, s, b, n):
    c, _, _ = counts(e, n, (g.items, g.acts, g.dves, 8, 4, 2 * NEWTON_OPS))
    for m in range(STEPS):
        pool_items(e, g, s, b, m, c)


def sequences(e, first_n, slot):
    slot(first_n, 0, 0, False, True, True, True)
    with e.Fori(0, (SEQS - 4) // 2) as i:
        for k in range(2):
            seq = e.snap(i * 2 + k + 1)
            slot(e.snap(first_n + seq), seq, 1 - k, True, True, True, True)
    for seq in range(SEQS - 3, SEQS + 1):
        slot(first_n + seq, seq, seq % 2, True, seq < SEQS, seq < SEQS - 1, seq < SEQS - 2)


def pe_attention(e, g, s, b, n):
    pe_first_items(e, g, s, b, n)
    sequences(e, n, lambda n, seq, par, prev, cur, nxt, inp: pe_slot(e, g, s, b, n, par, prev, cur, nxt))


def act_attention(e, g, s, b, n):
    act_first_items(e, g, s, b, n, 0)
    sequences(e, n, lambda n, seq, par, prev, cur, nxt, inp: act_slot(e, g, s, b, n, seq, par, prev, cur, nxt, inp))


def dve_attention(e, g, s, b, n):
    dve_first_items(e, g, s, b, n, 0)
    sequences(e, n, lambda n, seq, par, prev, cur, nxt, inp: dve_slot(e, g, s, b, n, seq, par, prev, cur, nxt, inp))


def pool_attention(e, g, s, b, n):
    pool_first_items(e, g, s, b, n)
    sequences(e, n, lambda n, seq, par, prev, cur, nxt, inp: pool_slot(e, g, s, b, n, prev, cur, nxt))



class FfnSems:

    def __init__(self, ctx, nc, tag):
        def sem(name):
            return ctx.enter_context(nc.semaphore(f"{tag}_{name}"))

        self.shifted = sem("shifted")
        self.mean = sem("mean")
        self.centred = sem("centred")
        self.squares = sem("squares")
        self.variance = sem("variance")
        self.newton = sem("newton")
        self.diag = sem("diag")
        self.rstd = sem("rstd")
        self.normed = sem("normed")
        self.affine = sem("affine")
        self.up_full = sem("up_full")
        self.gelu = sem("gelu")
        self.gated = sem("gated")
        self.down_full = sem("down_full")
        self.residual = sem("residual")


def pe_ffn_credit(e, s):
    e.sem_inc(s.mean, UNITS)
    e.sem_inc(s.variance, UNITS)
    e.sem_inc(s.rstd, UNITS)
    e.sem_inc(s.up_full, NF * UNITS)
    e.sem_inc(s.down_full, UNITS)


def act_ffn_credit(e, s):
    e.sem_inc(s.shifted, UNITS)
    e.sem_inc(s.affine, UNITS)
    e.sem_inc(s.gelu, NF * UNITS)


def dve_ffn_credit(e, s):
    e.sem_inc(s.centred, UNITS)
    e.sem_inc(s.newton, 2 * (NEWTON_OPS + 1))
    e.sem_inc(s.diag, UNITS)
    e.sem_inc(s.normed, UNITS)
    e.sem_inc(s.gated, NF * UNITS)
    e.sem_inc(s.residual, UNITS)


def pool_ffn_credit(e, s):
    e.sem_inc(s.squares, UNITS)


def unit(a, u):
    return a[:, bass.ds(u * UNIT, UNIT)]


def norm_source(b, plain, u):
    return unit(b.X1, u) if plain else b.xs[:, u % 2, :]


def stats_act(e, s, b, layer):
    base = layer * UNITS + UNITS
    for u in range(UNITS):
        e.wait_ge(s.centred, base + u - 1)
        e.activation(b.xs[0:64, u % 2, :], b.X[0:64, u * UNIT:(u + 1) * UNIT], ACT.Copy)
        dst = b.xs[64:P, u % 2, :].rearrange("p (q t) -> p q t", t=N_TOK)
        src = b.X[64:P, u * UNIT:(u + 1) * UNIT].rearrange("p (q t) -> p q t", t=N_TOK)
        e.activation(dst[:, :, 1:N_TOK], src[:, :, 0:N_TOK - 1], ACT.Copy).then_inc(s.shifted, 1)


def stats_pe(e, s, b, base, plain):
    for u in range(UNITS + 1):
        if u < UNITS:
            if not plain:
                e.wait_ge(s.shifted, base + u + 1)
            e.wait_ge(s.centred, base + u - 1)
            e.matmul(b.bank[u % 2][:, :], b.inv_dim[:, :], norm_source(b, plain, u), start=True, stop=True).then_inc(s.mean, 1)
        if u == UNITS:
            norm_pe(e, s, b, base, 0)
            norm_pe(e, s, b, base + 1, 1)
        if u >= 1:
            e.wait_ge(s.squares, base + u)
            for t in range(4):
                v = 4 * (u - 1) + t
                mm = e.matmul(variances(b, 0 if u - 1 < UNITS // 2 else 1)[:, v:v + 1], b.sqc[:, (u - 1) % 2, P * t:P * (t + 1)], b.inv_dim[:, 0:1],
                              start=True, stop=True)
            mm.then_inc(s.variance, 1)


def variances(b, half):
    return b.bank[5 + half]


def stats_dve(e, s, b, base, base_newton, plain, dst):
    for u in range(UNITS):
        e.wait_ge(s.mean, base + u + 1)
        if u == 0:
            e.wait_ge(s.normed, base + 0)
        e.tensor_tensor(unit(b.xc, u), norm_source(b, plain, u), b.bank[u % 2][:, :], ALU.subtract).then_inc(s.centred, 1)
        if u >= UNITS - 3:
            for i in range(4):
                rstd_dve(e, s, b, base, base_newton, 0, 4 * (u - UNITS + 3) + i)
    norm_dve_diag(e, s, b, base, base_newton + NEWTON_OPS + 1, 0, 0)
    norm_dve_diag(e, s, b, base + 1, base_newton + NEWTON_OPS + 1, 1, 1)
    norm_dve(e, s, b, base, 0, 0, dst)
    for i in range(NEWTON_OPS + 1):
        rstd_dve(e, s, b, base, base_newton, 1, i)


def stats_pool(e, s, b, base):
    for u in range(UNITS):
        e.wait_ge(s.centred, base + u + 1)
        e.wait_ge(s.variance, base + u - 1)
        e.tensor_tensor(b.sqc[:, u % 2, :], unit(b.xc, u), unit(b.xc, u), ALU.mult).then_inc(s.squares, 1)


def rstd_dve(e, s, b, base, base_newton, half, i):
    cols = slice(2 * UNITS * half, 2 * UNITS * (half + 1))
    e.wait_ge(s.newton, base_newton + (NEWTON_OPS + 1) * half + i)
    if i == 0:
        e.wait_ge(s.variance, base + UNITS // 2 * (half + 1))
        e.tensor_scalar(b.var[:, cols], variances(b, half)[:, cols], LN_EPS, None, ALU.add).then_inc(s.newton, 1)
    else:
        rsqrt_op(e, i - 1, b.nx[:, cols], b.rstd[:, cols], b.na[:, cols], b.var[:, cols], 0.0, 1.0).then_inc(s.newton, 1)


def norm_dve_diag(e, s, b, base, base_newton, u, par):
    e.wait_ge(s.newton, base_newton)
    e.wait_ge(s.rstd, base - 1)
    e.tensor_tensor(b.diag[:, par, :, :], b.ident[:, :].unsqueeze(1).broadcast_to([P, 4, P]),
                    b.rstd[:, bass.ds(u * 4, 4)].unsqueeze(2).broadcast_to([P, 4, P]), ALU.mult).then_inc(s.diag, 1)


def norm_pe(e, s, b, base, par):
    e.wait_ge(s.diag, base + 1)
    e.wait_ge(s.normed, base - 1)
    e.matmul(b.bank[7 * par][:, :], b.ones[:, :], b.diag[:, par, :, :].rearrange("p a b -> p (a b)"), start=True, stop=True).then_inc(s.rstd, 1)


def norm_dve(e, s, b, base, u, par, dst):
    e.wait_ge(s.rstd, base + 1)
    e.tensor_tensor(unit(dst, u), unit(b.xc, u), b.bank[7 * par][:, :], ALU.mult).then_inc(s.normed, 1)


def affine_act(e, s, b, base, base3, u, par):
    e.wait_ge(s.normed, base + 1)
    e.wait_ge(s.up_full, base3 - NF)
    e.activation(b.xn[:, par, :], unit(b.xc, u), ACT.Identity, bias=b.vec[:, 1:2], scale=b.vec[:, 0:1]).then_inc(s.affine, 1)


def up_pe(e, s, b, base, base3, par):
    e.wait_ge(s.affine, base + 1)
    for c, (at, size) in enumerate(F_CHUNKS):
        ring = (par + c) % 2
        e.wait_ge(s.gated, base3 + c - 1)
        for k, off in enumerate((DIM_INNER, 0)):
            mm = e.matmul(b.bank[1 + 2 * ring + k][0:size, :], b.w1[:, off + at:off + at + size], b.xn[:, par, :],
                          start=True, stop=True)
        mm.then_inc(s.up_full, 1)


def gelu_act(e, s, b, base3, par):
    for c, (at, size) in enumerate(F_CHUNKS):
        ring = (par + c) % 2
        e.wait_ge(s.up_full, base3 + c + 1)
        e.wait_ge(s.gated, base3 + c - 1)
        e.activation(b.ge[0:size, ring, :], b.bank[1 + 2 * ring][0:size, :], ACT.Gelu,
                     bias=b.vec[0:size, 5 + c:6 + c]).then_inc(s.gelu, 1)


def gate_dve(e, s, b, base, base3, par):
    e.wait_ge(s.down_full, base - 1)
    for c, (at, size) in enumerate(F_CHUNKS):
        ring = (par + c) % 2
        e.wait_ge(s.gelu, base3 + c + 1)
        e.scalar_tensor_tensor(b.h[0:size, par, c, :], b.bank[2 + 2 * ring][0:size, :], b.vec[0:size, 2 + c:3 + c],
                               b.ge[0:size, ring, :], ALU.add, ALU.mult).then_inc(s.gated, 1)


def down_pe(e, s, b, base, base3, par):
    e.wait_ge(s.gated, base3 + NF)
    e.wait_ge(s.residual, base - 1)
    for c, (at, size) in enumerate(F_CHUNKS):
        mm = e.matmul(b.bank[5 + par][:, :], b.w2[0:size, c, :], b.h[0:size, par, c, :], start=(c == 0), stop=(c == NF - 1))
    mm.then_inc(s.down_full, 1)


def down_dve(e, s, b, base, u, par):
    e.wait_ge(s.down_full, base + 1)
    x = unit(b.X, u)
    e.scalar_tensor_tensor(x, b.bank[5 + par][:, :], b.vec[:, 8:9], x, ALU.add, ALU.add).then_inc(s.residual, 1)


def ffn_units(e, base, step):
    def at(u):
        return e.snap(base + u), e.snap(base * NF + u * NF)

    step(0, 0, at, 0)
    with e.Fori(0, (UNITS - 4) // 2) as i:
        for k in range(2):
            step(e.snap(i * 2 + k + 1), 1 - k, at, 1)
    for u in range(UNITS - 3, UNITS + 1):
        step(u, u % 2, at, u)


def pe_ffn(e, s, b, base):
    def step(u, par, at, k):
        if k < UNITS:
            up_pe(e, s, b, *at(u), par)
        if k + 2 < UNITS:
            norm_pe(e, s, b, at(e.snap(u + 2))[0], par)
        if k >= 1:
            down_pe(e, s, b, *at(e.snap(u - 1)), 1 - par)

    ffn_units(e, base, step)


def act_ffn(e, s, b, base):
    affine_act(e, s, b, e.snap(base), e.snap(base * NF), 0, 0)

    def step(u, par, at, k):
        if k + 1 < UNITS:
            v = e.snap(u + 1)
            affine_act(e, s, b, *at(v), v, 1 - par)
        if k < UNITS:
            gelu_act(e, s, b, at(u)[1], par)

    ffn_units(e, base, step)


def dve_ffn(e, s, b, base, base_newton):
    def step(u, par, at, k):
        if k + 1 < UNITS:
            v = e.snap(u + 1)
            norm_dve(e, s, b, at(v)[0], v, 1 - par, b.xc)
        if k + 2 < UNITS:
            v = e.snap(u + 2)
            norm_dve_diag(e, s, b, at(v)[0], base_newton, v, par)
        if k < UNITS:
            gate_dve(e, s, b, *at(u), par)
        if k >= 1:
            v = e.snap(u - 1)
            down_dve(e, s, b, at(v)[0], v, 1 - par)

    ffn_units(e, base, step)



def build(nc, x_t, w0, wo0, vec0, vbias, masks, ident, inv_dim, ones, rope, rowmask, wqkv, qks, wo, w1, w2, vecs, out_t):
    with ExitStack() as ctx:
        def sb(name, shape, dt=F32):
            return ctx.enter_context(nc.sbuf_tensor(name, shape, dt))

        def sem(name):
            return ctx.enter_context(nc.semaphore(name))

        b = Buffers()
        b.bank = [ctx.enter_context(nc.psum_tensor(f"bank{i}", [P, 512], F32)) for i in range(8)]
        b.work, b.scores, b.pt, b.out = b.bank[0:3], b.bank[3:5], b.bank[5:7], b.bank[7]

        b.X = sb("x_stream", [P, TOKENS])
        b.X1 = sb("x_outer", [P, TOKENS])
        W_ATT = 3 * INNER + INNER
        watt_f = sb("watt_f32", [P, W_ATT])
        watt = [sb(f"watt_{k}", [P, W_ATT], BF16) for k in ("hi", "lo")]
        wffn = sb("wffn", [P, 2 * DIM_INNER + NF * DIM])
        b.wh, b.wl = (w[:, 0:3 * INNER] for w in watt)
        b.woh, b.wol = (w[:, 3 * INNER:].rearrange("p (c d) -> p c d", c=INNER // P) for w in watt)
        b.w1 = wffn[:, 0:2 * DIM_INNER]
        b.w2 = wffn[:, 2 * DIM_INNER:].rearrange("p (c d) -> p c d", c=NF)
        w0_sb = sb("w_first", [P, 4 * DIM])
        b.w0, b.wo0 = w0_sb[:, 0:3 * DIM], w0_sb[:, 3 * DIM:]

        b.ident, b.inv_dim, b.ones = sb("ident", [P, P]), sb("inv_dim", [P, P]), sb("ones", [P, P])
        b.identb = sb("identb", [P, P], BF16)
        maskf = wffn[:, 0:5 * BLOCK_K].rearrange("p (m k) -> p m k", m=5)
        b.maskb = sb("maskb", [P, 5, BLOCK_K], BF16)
        b.mask_of = lambda g, t: t if g.first else 2 + t
        rope_sb = sb("rope", [P, 2, 4, DIM_HEAD])
        qks_sb = sb("qks", [P, 4, DIM_HEAD])
        b.table = sb("table", [P, 2, 4, DIM_HEAD])
        b.rowmask = sb("rowmask", [P, 4])
        b.qkb = sb("bias0", [P, 3])
        b.vbias = sb("vbias0", [BLOCK_K, DIM])
        vecs_sb = sb("vecs", [P, DEPTH, 9])
        b.vec = sb("vec", [P, 9])

        qbuf = sb("qbuf", [P, 2 * 2 * 8 * N_TOK // 2])
        kbuf = sb("kbuf", [P, 2 * 2 * 8 * PADDED], BF16)
        vbuf = sb("vbuf", [P, 2 * BLOCKS * INNER])
        q4 = qbuf[:, :].bitcast(BF16).rearrange("p (h a s t) -> p h a s t", h=2, a=2, s=8)
        b.qh, b.ql = q4[:, 0], q4[:, 1]
        k4 = kbuf[:, :].rearrange("p (h a s t) -> p h a s t", h=2, a=2, s=8)
        b.kh, b.kl = k4[:, 0], k4[:, 1]
        b.v = vbuf[0:BLOCK_K, :].rearrange("p (a s t) -> p a s t", a=2, s=BLOCKS)
        b.q0 = qbuf[:, 0:2 * 4 * N_TOK].rearrange("p (a s t) -> p a s t", a=2, s=4)
        b.k0 = kbuf[:, :].bitcast(F32)[:, 0:2 * PADDED].rearrange("p (a t) -> p a t", a=2)

        rotbuf = sb("rotbuf", [P, 8 * 512])
        b.rot = rotbuf[:, :].rearrange("p (s d) -> p s d", s=8)
        mbuf = sb("mbuf", [P, 4 * 512])
        m4 = mbuf[:, :].rearrange("p (k s d) -> p k s d", k=2, s=2)
        b.m1, b.m2 = m4[:, 0], m4[:, 1]
        b.sq = sb("sq", [P, 2, 512])
        b.ss = sb("ss", [P, 2, 4 * HEADS])
        b.nx, b.na = sb("newton_x", [P, 4 * HEADS]), sb("newton_a", [P, 4 * HEADS])
        b.rk, b.rq = sb("rk", [P, 2 * HEADS]), sb("rq", [P, 2, 2 * HEADS])
        b.rmax, b.nmax = sb("rmax", [P, 2, 4]), sb("nmax", [P, 2, 4])
        b.den, b.rden = sb("den", [P, 4, 4]), sb("rden", [P, 4, 4])
        b.probs = sb("probs", [P, 4, 4, BLOCK_K])
        b.ptf = sb("probs_t", [BLOCK_K, 2, 512])
        otbuf = sb("outs_t", [P, 8 * N_TOK])
        b.oth, b.otl = (otbuf[:, 4 * N_TOK * k:4 * N_TOK * (k + 1)].bitcast(BF16).rearrange("p (c t) -> p c t", c=8)
                        for k in range(2))
        b.ot = otbuf[:, 0:N_TOK]
        xbuf = sb("inputs", [P, 2 * PADDED])
        b.xh, b.xl = (xbuf[:, PADDED * k:PADDED * (k + 1)].bitcast(BF16).rearrange("p (a t) -> p a t", a=2)
                      for k in range(2))
        b.x0 = xbuf[:, :].rearrange("p (a t) -> p a t", a=2)
        b.qbias = sb("qbias0", [P, 4])

        def pair(a, at, n=2):
            return a[:, at:at + n * UNIT].rearrange("p (s t) -> p s t", s=n)

        b.xc = vbuf[:, 0:TOKENS]
        b.xn = pair(vbuf, TOKENS)
        b.xs = pair(qbuf, 0)
        b.sqc = pair(qbuf, 2 * UNIT)
        b.ge = pair(qbuf, 2 * UNIT)
        b.diag = pair(mbuf, 2 * UNIT).rearrange("p s (a t) -> p s a t", a=4)
        b.h = rotbuf[:, 0:2 * NF * UNIT].rearrange("p (s c t) -> p s c t", s=2, c=NF)
        b.var, b.rstd = sb("var", [P, 4 * UNITS]), sb("rstd", [P, 4 * UNITS])

        g0, g1 = Geometry(True), Geometry(False)

        loaded, att_loaded, ffn_loaded = sem("loaded"), sem("att_loaded"), sem("ffn_loaded")
        loads = [(b.X1[:, :], x_t), (b.ident[:, :], ident), (b.inv_dim[:, :], inv_dim), (b.ones[:, :], ones),
                 (maskf[:, :, :], masks), (rope_sb[:, :, :, :], rope), (b.rowmask[:, :], rowmask), (b.qkb[:, :], vec0),
                 (b.vbias[:, :], vbias), (vecs_sb[:, :, :], vecs), (b.w0, w0), (b.wo0, wo0)]
        with nc.Block() as block:
            @block.sync
            def _(sp):
                for dst, src in loads:
                    sp.dma_start(dst, src).then_inc(loaded, 16)

            @block.gpsimd
            def _(pool):
                pool.memset(kbuf[:, :], 0.0)
                pool.memset(xbuf[:, :], 0.0)

            @block.vector
            def _(dve):
                dve.wait_ge(loaded, 16 * len(loads))
                dve.tensor_copy(b.identb[:, :], b.ident[:, :])
                dve.tensor_copy(b.maskb[:, :, :], maskf)
                dve.tensor_tensor(b.qbias[:, :], b.rowmask[:, :], b.qkb[:, 0:1].broadcast_to([P, 4]), ALU.mult)

        def load_attention_weights(sp, layer):
            sp.dma_start(watt_f[:, 0:3 * INNER], wqkv[layer, :, :].rearrange("a p d -> p (a d)")).then_inc(att_loaded, 16)
            sp.dma_start(watt_f[:, 3 * INNER:].rearrange("p (c d) -> p c d", c=INNER // P),
                         wo[layer, :, :].rearrange("a (c p) d -> p (a c) d", p=P)).then_inc(att_loaded, 16)
            sp.dma_start(qks_sb[:, :, :], qks[layer, :, :, :].rearrange("a p k d -> p (a k) d")).then_inc(att_loaded, 16)

        def load_ffn_weights(sp, layer):
            sp.dma_start(wffn[:, 0:2 * DIM_INNER], w1[layer, :, :].rearrange("a p d -> p (a d)")).then_inc(ffn_loaded, 16)
            sp.dma_start(b.w2, w2[layer, :, :].rearrange("a (c p) d -> p (a c) d", p=P)).then_inc(ffn_loaded, 16)

        w_hi, w_ready = sem("w_hi"), sem("w_ready")

        def split_weights(pool, layer):
            pool.wait_ge(att_loaded, layer * 48 + 48)
            if not isinstance(layer, int):
                pool.wait_ge(s1.residual, layer * SEQS + FIRST_N)
            pool.tensor_tensor(b.table[:, :, :, :], rope_sb[:, :, :, :],
                               qks_sb[:, :, :].unsqueeze(1).broadcast_to([P, 2, 4, DIM_HEAD]), ALU.mult)
            pool.tensor_copy(watt[0][:, :], watt_f[:, :]).then_inc(w_hi, 1)
            pool.wait_ge(w_hi, layer + 1)
            pool.tensor_tensor(watt[1][:, :], watt_f[:, :], watt[0][:, :], ALU.subtract).then_inc(w_ready, 1)

        def layer_norm(tag, with_split):
            s = FfnSems(ctx, nc, tag)
            with nc.Block() as block:
                @block.tensor
                def _(pe):
                    pe_ffn_credit(pe, s)
                    stats_pe(pe, s, b, UNITS, True)
                    for u in range(2, UNITS):
                        norm_pe(pe, s, b, UNITS + u, u % 2)

                @block.scalar
                def _(act):
                    act.sem_inc(s.squares, UNITS)
                    for u in range(UNITS):
                        act.wait_ge(s.centred, UNITS + u + 1)
                        act.wait_ge(s.variance, UNITS + u - 1)
                        act.activation(b.sqc[:, u % 2, :], unit(b.xc, u), ACT.Square).then_inc(s.squares, 1)

                if with_split:
                    @block.gpsimd
                    def _(pool):
                        split_weights(pool, 0)

                @block.vector
                def _(dve):
                    dve_ffn_credit(dve, s)
                    ready = 2 * (2 * (NEWTON_OPS + 1))
                    stats_dve(dve, s, b, UNITS, ready // 2, True, b.X)
                    for u in range(1, UNITS):
                        if u + 1 < UNITS:
                            norm_dve_diag(dve, s, b, UNITS + u + 1, ready, u + 1, (u + 1) % 2)
                        norm_dve(dve, s, b, UNITS + u, u, u % 2, b.X)

        layer_norm("ln0", False)
        with nc.Block() as block:
            @block.vector
            def _(dve):
                dve.memset(vbuf[:, :], 0.0)
        s0 = AttentionSems(ctx, nc, "first")
        with nc.Block() as block:
            @block.sync
            def _(sp):
                load_attention_weights(sp, bass.ds(0, 1))

            @block.tensor
            def _(pe):
                pe_credit(pe, g0, s0)
                pe_attention(pe, g0, s0, b, FIRST_N)

            @block.scalar
            def _(act):
                act_credit(act, g0, s0)
                act_attention(act, g0, s0, b, FIRST_N)

            @block.vector
            def _(dve):
                dve_credit(dve, g0, s0)
                dve_attention(dve, g0, s0, b, FIRST_N)

            @block.gpsimd
            def _(pool):
                pool_credit(pool, g0, s0)
                pool_attention(pool, g0, s0, b, FIRST_N)
        s1 = AttentionSems(ctx, nc, "deep")
        layer_norm("ln1", True)

        f1 = FfnSems(ctx, nc, "ffn")
        vec_ready, xs_zero = sem("vec_ready"), sem("xs_zero")
        with nc.Block() as block:
            @block.vector
            def _(dve):
                dve.memset(kbuf[:, :], 0.0)
                dve.memset(xbuf[:, :], 0.0)
        with nc.Block() as block:
            @block.sync
            def _(sp):
                with sp.Fori(0, DEPTH - 1) as l:
                    sp.wait_ge(f1.residual, l * UNITS + UNITS)
                    load_ffn_weights(sp, bass.ds(l, 1))
                    sp.wait_ge(w_ready, l + 1)
                    load_attention_weights(sp, bass.ds(l + 1, 1))
                sp.wait_ge(f1.residual, DEPTH * UNITS)
                load_ffn_weights(sp, bass.ds(DEPTH - 1, 1))

            @block.tensor
            def _(pe):
                pe_credit(pe, g1, s1)
                pe_ffn_credit(pe, f1)
                with pe.Fori(0, DEPTH) as l:
                    pe.wait_ge(w_ready, l + 1)
                    pe_attention(pe, g1, s1, b, pe.snap(l * SEQS + FIRST_N))
                    base = pe.snap(l * UNITS + UNITS)
                    stats_pe(pe, f1, b, base, False)
                    pe.wait_ge(ffn_loaded, l * 32 + 32)
                    pe_ffn(pe, f1, b, base)

            @block.scalar
            def _(act):
                act_credit(act, g1, s1)
                act_ffn_credit(act, f1)
                with act.Fori(0, DEPTH) as l:
                    act.wait_ge(f1.residual, l * UNITS + UNITS)
                    act_attention(act, g1, s1, b, act.snap(l * SEQS + FIRST_N))
                    act.wait_ge(s1.residual, l * SEQS + SEQS + FIRST_N)
                    act.activation(b.xs[64:P, :, :].rearrange("p s (q t) -> p (s q) t", t=N_TOK)[:, :, 0:1],
                                   b.ident[64:P, 0:4].unsqueeze(2), ACT.Copy, scale=0.0).then_inc(xs_zero, 1)
                    stats_act(act, f1, b, l)
                    act.wait_ge(vec_ready, l + 1)
                    act_ffn(act, f1, b, act.snap(l * UNITS + UNITS))

            @block.vector
            def _(dve):
                dve_credit(dve, g1, s1)
                dve_ffn_credit(dve, f1)
                with dve.Fori(0, DEPTH) as l:
                    dve.wait_ge(f1.residual, l * UNITS + UNITS)
                    dve.tensor_copy(b.vec[:, :], vecs_sb[:, bass.ds(l, 1), :].rearrange("p a v -> p (a v)")).then_inc(vec_ready, 1)
                    dve.wait_ge(w_ready, l + 1)
                    dve_attention(dve, g1, s1, b, dve.snap(l * SEQS + FIRST_N))
                    base = dve.snap(l * UNITS + UNITS)
                    base_newton = dve.snap(l * (2 * (NEWTON_OPS + 1)) + 2 * (NEWTON_OPS + 1))
                    stats_dve(dve, f1, b, base, base_newton, False, b.xc)
                    dve.wait_ge(vec_ready, l + 1)
                    dve_ffn(dve, f1, b, base, dve.snap(base_newton + 2 * (NEWTON_OPS + 1)))

            @block.gpsimd
            def _(pool):
                pool_credit(pool, g1, s1)
                pool_ffn_credit(pool, f1)
                with pool.Fori(0, DEPTH - 1) as l:
                    pool_attention(pool, g1, s1, b, pool.snap(l * SEQS + FIRST_N))
                    stats_pool(pool, f1, b, pool.snap(l * UNITS + UNITS))
                    split_weights(pool, pool.snap(l + 1))
                pool_attention(pool, g1, s1, b, (DEPTH - 1) * SEQS + FIRST_N)
                stats_pool(pool, f1, b, DEPTH * UNITS)

        summed, stored = sem("summed"), sem("stored")
        with nc.Block() as block:
            @block.vector
            def _(dve):
                for u in range(UNITS):
                    dve.tensor_tensor(unit(b.X1, u), unit(b.X1, u), unit(b.X, u), ALU.add).then_inc(summed, 1)

            @block.sync
            def _(sp):
                for u in range(UNITS):
                    sp.wait_ge(summed, u + 1)
                    sp.dma_start(unit(out_t, u), unit(b.X1, u)).then_inc(stored, 16)
                sp.wait_ge(stored, 16 * UNITS)


def constants():
    f = np.float32
    big = -1e30
    q, k = np.arange(BLOCK_Q)[:, None], np.arange(BLOCK_K)[None, :]
    masks = np.zeros((P, 5, BLOCK_K), f)
    for t in range(2):
        for half in range(2):
            blk = 2 * t + half
            rows = slice(64 * half, 64 * half + 64)
            pos = 64 * blk + k - 16
            lo = 32 * (q // 32)
            ok = (k >= lo) & (k < lo + 64) & (pos >= 0) & (pos < N_TOK)
            masks[rows, t] = np.where(ok, 0.0, big)
            i, j = 64 * blk + q, 64 * blk + k - 32
            same = (j // 32 == i // 32) | (j // 32 == i // 32 - 1)
            ok = same & (j >= 0) & (i >= j) & (i <= j + 32)
            masks[rows, 2 + t] = np.where(ok, 0.0, big)
    half = np.arange(0, DIM_HEAD, 2, dtype=f)
    inv_freq = (f(1.0) / f(10000.0) ** (half / f(DIM_HEAD))).astype(f)
    t = np.arange(N_TOK, dtype=f)
    freqs = t[:, None] * inv_freq[None, :]
    base = ((half + f(0.4 * DIM_HEAD)) / f(1.4 * DIM_HEAD)).astype(f)
    power = (t - N_TOK // 2) / f(WINDOW // 2)
    scale = (base[None, :].astype(np.float64) ** power[:, None]).astype(f)
    cos, sin = np.cos(freqs.astype(np.float64)), np.sin(freqs.astype(np.float64))
    tabs = []
    for sc in (scale.astype(np.float64), 1.0 / scale.astype(np.float64)):
        tabs.append(np.concatenate([cos * sc, cos * sc], 1))
        tabs.append(np.concatenate([-sin * sc, sin * sc], 1))
    rope = np.stack(tabs, 1).astype(f).reshape(2, P, 4, DIM_HEAD).transpose(1, 0, 2, 3)
    rowmask = (np.arange(P)[:, None] % 32 // HEAD_DIM0 == np.arange(4)[None, :]).astype(f)
    return masks, np.eye(P, dtype=f), np.full((P, P), 1.0 / DIM, f), np.ones((P, P), f), rope, rowmask


def kernel(L0_attn_x, L0_attn_w_qkv, L0_attn_b_qkv, L0_attn_w_proj, L0_attn_b_proj, L0_ffn_Wqkv,
           L0_ffn_q_scale, L0_ffn_k_scale, L0_ffn_Wo, L0_ffn_ln_g, L0_ffn_ln_b, L0_ffn_W1, L0_ffn_b1,
           L0_ffn_W2, L0_ffn_b2):
    import concourse.bacc as bacc
    from concourse.bass_utils import run_bass_kernel_spmd

    def arr(a):
        return np.ascontiguousarray(np.asarray(a))

    masks, ident, inv_dim, ones, rope, rowmask = constants()
    x = arr(L0_attn_x)
    bq = arr(L0_attn_b_qkv)
    qs, ks = arr(L0_ffn_q_scale), arr(L0_ffn_k_scale)
    swap = np.roll(np.arange(DIM_HEAD), DIM_HEAD // 2)
    qks = np.stack([qs, qs[:, swap], ks, ks[:, swap]], 1)[:, None]
    b1 = arr(L0_ffn_b1)
    b1p = np.zeros((DEPTH, 2, NF * P), b1.dtype)
    b1p[:, :, :DIM_INNER] = b1.reshape(DEPTH, 2, DIM_INNER)
    w2 = arr(L0_ffn_W2)
    w2p = np.zeros((DEPTH, NF * P, DIM), w2.dtype)
    w2p[:, :DIM_INNER] = w2
    vecs = np.concatenate([arr(L0_ffn_ln_g)[:, None], arr(L0_ffn_ln_b)[:, None],
                           b1p.reshape(DEPTH, 2 * NF, P), arr(L0_ffn_b2)[:, None]], 1)
    arrays = {
        "x_t": x.reshape(TOKENS, DIM).T, "w0": arr(L0_attn_w_qkv).T, "wo0": arr(L0_attn_w_proj).T,
        "vec0": np.stack([bq[:DIM], bq[DIM:2 * DIM], arr(L0_attn_b_proj)], 1),
        "vbias": np.broadcast_to(bq[2 * DIM:], (BLOCK_K, DIM)), "masks": masks, "ident": ident,
        "inv_dim": inv_dim, "ones": ones, "rope": rope, "rowmask": rowmask, "wqkv": arr(L0_ffn_Wqkv),
        "qks": np.broadcast_to(qks, (DEPTH, P, 4, DIM_HEAD)), "wo": arr(L0_ffn_Wo), "w1": arr(L0_ffn_W1),
        "w2": w2p, "vecs": vecs.transpose(2, 0, 1),
    }
    arrays = {k: np.ascontiguousarray(v) for k, v in arrays.items()}
    nc = bacc.Bacc("TRN2", target_bir_lowering=False, num_devices=1)
    args = {k: nc.dram_tensor(f"in_{k}", v.shape, mybir.dt.from_np(v.dtype), kind="ExternalInput").ap()
            for k, v in arrays.items()}
    out = nc.dram_tensor("out_t", (DIM, TOKENS), F32, kind="ExternalOutput").ap()
    build(nc, **args, out_t=out)
    r = run_bass_kernel_spmd(nc, [{f"in_{k}": v for k, v in arrays.items()}], core_ids=[0])
    return r.results[0]["out_t"].T.reshape(x.shape)
```
